# Optimizing a Trainium2 kernel written in Bass

```python
import numpy as np
import jax
import jax.numpy as jnp

def _softmax(x, axis=-1):
    return jax.nn.softmax(x, axis=axis)

def _gelu(x):
    return jax.nn.gelu(x, approximate=True)

def _silu(x):
    return jax.nn.silu(x)

def _sigmoid(x):
    return jax.nn.sigmoid(x)

def _layernorm(x, axis=-1, eps=1e-05):
    m = jnp.mean(x, axis=axis, keepdims=True)
    v = jnp.var(x, axis=axis, keepdims=True)
    return (x - m) / jnp.sqrt(v + eps)

def _scatter_add(tgt, idx, src, axis=0):
    return tgt.at[idx].add(src)

def _segment_sum(src, seg, n):
    return jax.ops.segment_sum(src, seg, n)
kernel_name = 'mk_xattn_ffn_d1_seqx_r4_3b887f'

def setup_inputs(seed: int=0):
    np.random.seed(seed)
    _w = jnp.asarray

    def _rec_inputs():
        import jax
        import jax.numpy as jnp
        _rk = jax.random.key(seed)
        x = 7.22e-05 + 1 * jax.random.normal(jax.random.fold_in(_rk, 1), (8, 512, 256), jnp.float32)
        _lenS = 512 - jax.random.randint(jax.random.fold_in(_rk, 7), (8,), 0, max(1, 512 // 4) + 1, jnp.int32)
        _lenS2 = 1024 - jax.random.randint(jax.random.fold_in(_rk, 8), (8,), 0, max(1, 1024 // 4) + 1, jnp.int32)
        _ctx_1024P = jax.random.normal(jax.random.fold_in(_rk, 11), (8, 16, 256), jnp.float32)
        _ctx_1024c = jax.random.dirichlet(jax.random.fold_in(_rk, 511), 0.3 * jnp.ones((16,), jnp.float32), (8, 1024))
        _ctx_1024t = jnp.einsum('bsk,bkd->bsd', _ctx_1024c, _ctx_1024P)
        _ctx_1024t = _ctx_1024t * jax.lax.rsqrt(jnp.mean(jnp.square(_ctx_1024t)) + 1e-12) * 0.953939
        ctx_1024 = -1.39393e-06 + 0.999914 * (_ctx_1024t + 0.3 * jax.random.normal(jax.random.fold_in(_rk, 611), (8, 1024, 256), jnp.float32))
        _validS = jnp.arange(512)[None, :] < _lenS[:, None]
        _validS2 = jnp.arange(1024)[None, :] < _lenS2[:, None]
        _causal = jnp.tril(jnp.ones((512, 512), dtype=bool))
        mask_BxS2_bf1 = jnp.ones((8, 1024), dtype=bool)
        return (x, ctx_1024, mask_BxS2_bf1)
    x, ctx_1024, mask_BxS2_bf1 = _rec_inputs()

    def _L0_xattn_setup():
        import jax, jax.numpy as jnp
        import numpy as np
        HEADS = 16
        DIM_HEAD = 64
        SCALE = DIM_HEAD ** (-0.5)
        key = jax.random.key(seed)
        ks = jax.random.split(key, 6)
        B, Nq, Nkv, D = (4, 512, 256, 256)
        inner = HEADS * DIM_HEAD
        return {'x': jax.random.normal(ks[0], (B, Nq, D), dtype=jnp.float32), 'context': jax.random.normal(ks[1], (B, Nkv, D), dtype=jnp.float32), 'mask': jnp.ones((B, Nkv), dtype=bool), 'Wq': jax.random.normal(ks[2], (inner, D), dtype=jnp.float32) * D ** (-0.5), 'Wkv': jax.random.normal(ks[3], (2 * inner, D), dtype=jnp.float32) * D ** (-0.5), 'Wout': jax.random.normal(ks[4], (D, inner), dtype=jnp.float32) * inner ** (-0.5), 'b_out': jnp.zeros((D,), dtype=jnp.float32)}
    _L0_xattn_all = _L0_xattn_setup()
    _L0_xattn_in = {k: v for k, v in _L0_xattn_all.items() if k in ('Wq', 'Wkv', 'Wout', 'b_out')}
    del _L0_xattn_all

    def _L0_ffn_setup():
        import jax, jax.numpy as jnp
        import numpy as np
        LN_EPS = 1e-05

        def layer_norm(x, g, b):
            mu = jnp.mean(x, axis=-1, keepdims=True)
            var = jnp.mean(jnp.square(x - mu), axis=-1, keepdims=True)
            return (x - mu) * jax.lax.rsqrt(var + LN_EPS) * g + b

        def ternary_quant(w):
            scale = 1.0 / jnp.clip(jnp.mean(jnp.abs(w)), 1e-05)
            wq = jnp.clip(jnp.round(w * scale), -1.0, 1.0) / scale
            return w + jax.lax.stop_gradient(wq - w)
        key = jax.random.key(seed)
        ks = jax.random.split(key, 3)
        dim, hidden = (256, 1024)
        B, S = (8, 256)
        x = jax.random.normal(ks[0], (B, S, dim), dtype=jnp.float32)
        w1 = jax.random.normal(ks[1], (hidden, dim), dtype=jnp.float32) * 0.02
        w2 = jax.random.normal(ks[2], (dim, hidden), dtype=jnp.float32) * 0.02
        return {'x': x, 'ln1_g': jnp.ones((dim,), jnp.float32), 'ln1_b': jnp.zeros((dim,), jnp.float32), 'w1': w1, 'b1': jnp.zeros((hidden,), jnp.float32), 'ln2_g': jnp.ones((hidden,), jnp.float32), 'ln2_b': jnp.zeros((hidden,), jnp.float32), 'w2': w2, 'b2': jnp.zeros((dim,), jnp.float32)}
    _L0_ffn_all = _L0_ffn_setup()
    _L0_ffn_in = {k: v for k, v in _L0_ffn_all.items() if k in ('ln1_g', 'ln1_b', 'w1', 'b1', 'ln2_g', 'ln2_b', 'w2', 'b2')}
    del _L0_ffn_all
    return {'x': x, 'ctx_1024': ctx_1024, 'mask_BxS2_bf1': mask_BxS2_bf1, 'L0_xattn_Wq': _L0_xattn_in['Wq'], 'L0_xattn_Wkv': _L0_xattn_in['Wkv'], 'L0_xattn_Wout': _L0_xattn_in['Wout'], 'L0_xattn_b_out': _L0_xattn_in['b_out'], 'L0_ffn_ln1_g': _L0_ffn_in['ln1_g'], 'L0_ffn_ln1_b': _L0_ffn_in['ln1_b'], 'L0_ffn_w1': _L0_ffn_in['w1'], 'L0_ffn_b1': _L0_ffn_in['b1'], 'L0_ffn_ln2_g': _L0_ffn_in['ln2_g'], 'L0_ffn_ln2_b': _L0_ffn_in['ln2_b'], 'L0_ffn_w2': _L0_ffn_in['w2'], 'L0_ffn_b2': _L0_ffn_in['b2']}

def reference(x, ctx_1024, mask_BxS2_bf1, L0_xattn_Wq, L0_xattn_Wkv, L0_xattn_Wout, L0_xattn_b_out, L0_ffn_ln1_g, L0_ffn_ln1_b, L0_ffn_w1, L0_ffn_b1, L0_ffn_ln2_g, L0_ffn_ln2_b, L0_ffn_w2, L0_ffn_b2):
    import jax
    import jax.numpy as jnp

    def _L0_xattn_ref(x, context, mask, Wq, Wkv, Wout, b_out):
        import jax, jax.numpy as jnp
        import numpy as np
        HEADS = 16
        DIM_HEAD = 64
        SCALE = DIM_HEAD ** (-0.5)
        B, Nq, _ = x.shape
        Nkv = context.shape[1]
        q = x @ Wq.T
        kv = context @ Wkv.T
        k, v = jnp.split(kv, 2, axis=-1)
        q = q.reshape(B, Nq, HEADS, DIM_HEAD).transpose(0, 2, 1, 3)
        k = k.reshape(B, Nkv, HEADS, DIM_HEAD).transpose(0, 2, 1, 3)
        v = v.reshape(B, Nkv, HEADS, DIM_HEAD).transpose(0, 2, 1, 3)
        sim = jnp.einsum('bhid,bhjd->bhij', q, k) * SCALE
        max_neg = -jnp.finfo(sim.dtype).max
        sim = jnp.where(mask[:, None, None, :], sim, max_neg)
        attn = jax.nn.softmax(sim, axis=-1)
        out = jnp.einsum('bhij,bhjd->bhid', attn, v)
        out = out.transpose(0, 2, 1, 3).reshape(B, Nq, HEADS * DIM_HEAD)
        return out @ Wout.T + b_out

    def _L0_ffn_ref(x, ln1_g, ln1_b, w1, b1, ln2_g, ln2_b, w2, b2):
        import jax, jax.numpy as jnp
        import numpy as np
        LN_EPS = 1e-05

        def layer_norm(x, g, b):
            mu = jnp.mean(x, axis=-1, keepdims=True)
            var = jnp.mean(jnp.square(x - mu), axis=-1, keepdims=True)
            return (x - mu) * jax.lax.rsqrt(var + LN_EPS) * g + b

        def ternary_quant(w):
            scale = 1.0 / jnp.clip(jnp.mean(jnp.abs(w)), 1e-05)
            wq = jnp.clip(jnp.round(w * scale), -1.0, 1.0) / scale
            return w + jax.lax.stop_gradient(wq - w)
        h = layer_norm(x, ln1_g, ln1_b)
        h = jnp.einsum('bsd,hd->bsh', h, ternary_quant(w1)) + b1
        h = jax.nn.gelu(h, approximate=False)
        h = layer_norm(h, ln2_g, ln2_b)
        out = jnp.einsum('bsh,dh->bsd', h, ternary_quant(w2)) + b2
        return out
    x = x + _L0_xattn_ref(_layernorm(x, axis=-1), ctx_1024, mask_BxS2_bf1, L0_xattn_Wq, L0_xattn_Wkv, L0_xattn_Wout, L0_xattn_b_out)
    x = x + _L0_ffn_ref(_layernorm(x, axis=-1), L0_ffn_ln1_g, L0_ffn_ln1_b, L0_ffn_w1, L0_ffn_b1, L0_ffn_ln2_g, L0_ffn_ln2_b, L0_ffn_w2, L0_ffn_b2)
    return x

_drawn_inputs = setup_inputs


def setup_inputs(seed=0):
    import zlib

    import numpy as np

    out = dict(_drawn_inputs(seed))
    spreads = {'L0_xattn_b_out': (0.0, 0.1),
     'L0_ffn_ln1_g': (1.0, 0.2),
     'L0_ffn_ln1_b': (0.0, 0.1),
     'L0_ffn_b1': (0.0, 0.1),
     'L0_ffn_ln2_g': (1.0, 0.2),
     'L0_ffn_ln2_b': (0.0, 0.1),
     'L0_ffn_b2': (0.0, 0.1)}
    factors = {}
    for name, (base, spread) in spreads.items():
        noise = np.random.default_rng([zlib.crc32(name.encode()), seed]).standard_normal(out[name].shape)
        drawn = base * np.exp(spread * noise) if base else spread * noise
        out[name] = jnp.asarray(drawn.astype(out[name].dtype))
    for name, factor in factors.items():
        out[name] = (out[name] * factor).astype(out[name].dtype)
    return out
```

```python
from contextlib import ExitStack

import concourse.bass as bass
from concourse import mybir

ALU = mybir.AluOpType
ACT = mybir.ActivationFunctionType
AXES = mybir.AxisListType
F32 = mybir.dt.float32
F32R = mybir.dt.float32r
BF16 = mybir.dt.bfloat16
U8 = mybir.dt.uint8

P = 128
B, NQ, NKV, D = 8, 512, 1024, 256
HEADS, DH = 16, 64
QT = NQ // P
DC = D // P
QUAD = 4
QUADS = HEADS // QUAD
STEPS = B * QUADS
SLOTS = QUAD * QT
KC = NKV // P
NH = NKV // 512
HID = 1024
HC = HID // P
EPS = 1e-5
MASKED = 3e38
LARGEST = 3.4e38
T_LAG, PV_LAG, U_LAG = 6, 7, 8

UNITS = {0: ("v", 0, 2), 1: ("v", 0, 3), 2: ("k", 0, 2), 3: ("k", 0, 3), 4: ("q", 0, 2), 5: ("q", 0, 3),
         8: ("o", -1, 0), 9: ("o", -1, 1), 10: ("k", 1, 0), 11: ("k", 1, 1), 12: ("q", 1, 0), 13: ("q", 1, 1),
         14: ("v", 1, 0), 15: ("v", 1, 1)}
PER_QUAD = {"k": 4, "q": 4, "v": 4, "o": 2}
JOBS = {0: [("wo", -1, 0)], 1: [("wo", -1, 1)], 3: [("vs", 0, 0)], 4: [("vs", 0, 1)], 5: [("wk", 1, 0)],
        6: [("ctx", 1, 0)], 7: [("ctx", 1, 1), ("wq", 1, 0)], 8: [("ctx", 1, 2)], 9: [("ctx", 1, 3)],
        10: [("xn", 1, 0)], 11: [("xn", 1, 1)], 12: [("wv", 1, 0)], 13: [("vs", 0, 2)], 14: [("vs", 0, 3)]}
PIECES = {"wo": 2, "wk": 1, "ctx": 4, "wq": 1, "xn": 2, "wv": 1, "vs": 4}
LOADS = [j for s in range(SLOTS) for j in JOBS.get(s, []) if j[0] != "vs"]
RAW = 4


def valid(i, dn):
    return not isinstance(i, int) or 0 <= i + dn < STEPS


def wait(eng, sem, i, per, off):
    if isinstance(i, int) and per * i + off <= 0:
        return
    eng.wait_ge(sem, per * i + off)


def stand_alone(eng, passed):
    eng.sem_inc(passed, 1)


def at_lag(s, lag):
    x = (s - lag) % SLOTS
    return (s - lag) // SLOTS, x // QT, x % QT


def run_loop(eng, body, first, last):
    for i in range(first, 1):
        body(i)
    with eng.Fori(1, STEPS - 1) as i:
        body(i)
    for i in range(STEPS - 1, last + 1):
        body(i)


def normalize_stage(nc, x, b_out, xnT, y):
    with ExitStack() as ctx:
        sb = lambda name, shape, dt=F32: ctx.enter_context(nc.sbuf_tensor(name, shape, dt))
        sem = lambda name: ctx.enter_context(nc.semaphore(name))
        rows = sb("n_rows", [P, 2, QT, D])
        xn = sb("n_xn", [P, 2, QT, D])
        yrow = sb("n_y", [P, 2, QT, D])
        xnt = sb("n_xnt", [P, 2, DC, NQ])
        bout = sb("n_bout", [P, D])
        ident = sb("n_ident", [P, P])
        half = sb("n_half", [P, QT])
        stats = sb("n_stats", [P, 2, QT, 6])
        mv = sb("n_mv", [P, 2, QT, 2])
        var = sb("n_var", [P, 2, QT])
        rstd = sb("n_rstd", [P, 2, QT])
        ps = ctx.enter_context(nc.psum_tensor("n_ps", [P, 2, DC, NQ], F32))
        loaded = [sem(f"n_loaded{u}") for u in range(2)]
        bias_in, const, ident0 = sem("n_bias_in"), sem("n_const"), sem("n_ident0")
        stat, aggr, vared, rstded = sem("n_stat"), sem("n_aggr"), sem("n_vared"), sem("n_rstd_s")
        normed, added, turned, copied = sem("n_normed"), sem("n_added"), sem("n_turned"), sem("n_copied")
        stored = [sem(f"n_stored{u}") for u in range(2)]
        passed = sem("n_passed")
        steps = B // 2
        with nc.Block() as block:
            @block.sync
            def _(sp):
                sp.dma_start(bout[:], b_out.unsqueeze(0).partition_broadcast(P)).then_inc(bias_in, 16)
                with sp.Fori(0, steps) as i:
                    for u in range(2):
                        sp.wait_ge(normed, 2 * i + u)
                        sp.wait_ge(added, 2 * i + u)
                        src = x[bass.ds(2 * i + u, 1)].rearrange("o (t p) d -> p (o t) d", p=P)
                        sp.dma_start(rows[:, u], src).then_inc(loaded[u], 16)
                for u in range(2):
                    sp.wait_ge(stored[u], 32 * steps)

            @block.gpsimd
            def _(pool):
                pool.memset(half[:], -0.5).then_inc(const, 1)
                pool.memset(ident[:], 0.0).then_inc(ident0, 1)
                pool.wait_ge(ident0, 1)
                pool.affine_select(out=ident[:], in_=ident[:], compare_op=ALU.not_equal, fill=1.0, base=0,
                                   pattern=[[-1, P]], channel_multiplier=1).then_inc(const, 1)
                pool.wait_ge(const, 1)
                pool.wait_ge(bias_in, 16)
                with pool.Fori(0, steps) as i:
                    for u in range(2):
                        pool.wait_ge(vared, 2 * i + u + 1)
                        pool.tensor_tensor(rstd[:, u], var[:, u], half[:], ALU.pow).then_inc(rstded, 1)
                        pool.wait_ge(stored[u], 32 * i)
                        for t in range(QT):
                            last = pool.tensor_tensor(yrow[:, u, t], rows[:, u, t], bout[:], ALU.add)
                        last.then_inc(added, 1)

            @block.vector
            def _(dve):
                with dve.Fori(0, steps) as i:
                    for u in range(2):
                        dve.wait_ge(loaded[u], 16 * i + 16)
                        for t in range(QT):
                            last = dve.bn_stats(stats[:, u, t], rows[:, u, t])
                        last.then_inc(stat, 1)
                        dve.wait_ge(stat, 2 * i + u + 1)
                        stand_alone(dve, passed)
                        for t in range(QT):
                            last = dve.bn_aggr(mv[:, u, t], stats[:, u, t])
                        last.then_inc(aggr, 1)
                        dve.wait_ge(aggr, 2 * i + u + 1)
                        dve.tensor_scalar(var[:, u], mv[:, u, :, 1], EPS, None, ALU.add).then_inc(vared, 1)
                        dve.wait_ge(rstded, 2 * i + u + 1)
                        dve.wait_ge(turned, 2 * i + u)
                        for t in range(QT):
                            last = dve.tensor_scalar(xn[:, u, t], rows[:, u, t], mv[:, u, t, 0:1],
                                                     rstd[:, u, t:t + 1], ALU.subtract, ALU.mult)
                        last.then_inc(normed, 1)

            @block.tensor
            def _(pe):
                pe.wait_ge(const, 2)
                with pe.Fori(0, steps) as i:
                    for u in range(2):
                        pe.wait_ge(normed, 2 * i + u + 1)
                        pe.wait_ge(copied, 2 * i + u)
                        for c in range(DC):
                            for t in range(QT):
                                last = pe.transpose(ps[:, u, c, t * P:(t + 1) * P],
                                                    xn[:, u, t, c * P:(c + 1) * P], ident[:])
                        last.then_inc(turned, 1)

            @block.scalar
            def _(act):
                with act.Fori(0, steps) as i:
                    for u in range(2):
                        act.wait_ge(turned, 2 * i + u + 1)
                        act.wait_ge(stored[u], 32 * i)
                        act.activation(xnt[:, u], ps[:, u], ACT.Copy).then_inc(copied, 1)
                        act.wait_ge(copied, 2 * i + u + 1)
                        act.dma_start(xnT[bass.ds(2 * i + u, 1)].rearrange("o p c q -> p (o c) q"),
                                      xnt[:, u]).then_inc(stored[u], 16)
                        act.wait_ge(added, 2 * i + u + 1)
                        act.dma_start(y[bass.ds(2 * i + u, 1)].rearrange("o p t d -> p (o t) d"),
                                      yrow[:, u]).then_inc(stored[u], 16)


def attention_stage(nc, ctxT, mask, wq, wk, wv, wo, xnT, y):
    with ExitStack() as ctx:
        sb = lambda name, shape, dt=F32: ctx.enter_context(nc.sbuf_tensor(name, shape, dt))
        sem = lambda name: ctx.enter_context(nc.semaphore(name))
        raw = sb("raw", [P, RAW, 512])
        ctx_hi, ctx_lo = (sb(f"ctx_{x}", [P, NH * DC, 512], F32R) for x in ("hi", "lo"))
        xn_hi, xn_lo = (sb(f"xn_{x}", [P, DC, NQ], F32R) for x in ("hi", "lo"))
        wq_hi, wq_lo = (sb(f"wq_{x}", [P, DC, QUAD, 2, DH], F32R) for x in ("hi", "lo"))
        wk_hi, wk_lo = (sb(f"wk_{x}", [P, DC, QUAD * DH], F32R) for x in ("hi", "lo"))
        wv_hi, wv_lo = (sb(f"wv_{x}", [P, DC, QUAD * DH], F32R) for x in ("hi", "lo"))
        wo_hi, wo_lo = (sb(f"wo_{x}", [P, QUAD, D], F32R) for x in ("hi", "lo"))
        q_hi, q_lo = (sb(f"q_{x}", [P, QUAD, NQ], F32R) for x in ("hi", "lo"))
        k_st = sb("k_stack", [P, QUAD, NKV], F32R)
        v_raw = sb("v_raw", [P, KC, QUAD, DH])
        v_st = sb("v_stack", [P, QUAD, KC, 2, DH], F32R)
        probs = sb("probs", [P, 2 * QT, NKV])
        pt_hi, pt_lo = (sb(f"pt_{x}", [P, 4, NQ], F32R) for x in ("hi", "lo"))
        u_hi, u_lo = (sb(f"u_{x}", [P, QUAD, NQ], F32R) for x in ("hi", "lo"))
        y_sb = sb("y_sb", [P, QT, D])
        mask_raw = sb("mask_raw", [P, NKV], U8)
        mask_bias = sb("mask_bias", [P, 2, NKV], BF16)
        low = sb("low", [P, SLOTS])
        rowsum, rinv = sb("rowsum", [P, SLOTS]), sb("rinv", [P, SLOTS])
        ident = sb("ident", [P, P])
        s_ps = ctx.enter_context(nc.psum_tensor("s_ps", [P, 2, NH, 512], F32))
        t_ps = ctx.enter_context(nc.psum_tensor("t_ps", [P, 2, NQ], F32))
        pv_ps = ctx.enter_context(nc.psum_tensor("pv_ps", [P, NQ], F32))
        m_ps = ctx.enter_context(nc.psum_tensor("m_ps", [P, 512], F32))

        ident0, ident_ready = sem("ident0"), sem("ident_ready")
        loaded = {j: sem(f"loaded_{j[0]}{j[2]}") for j in LOADS}
        split = {k: sem(f"split_{k}") for k in PIECES}
        unit = {k: sem(f"unit_{k}") for k in PER_QUAD}
        unit_hi = {k: sem(f"unit_hi_{k}") for k in "kq"}
        done = {k: sem(f"done_{k}") for k in PER_QUAD}
        k_lo_a = sem("k_lo_a")
        scored, masked, exped = sem("scored"), sem("masked"), sem("exped")
        inverted, normed = sem("inverted"), sem("normed")
        turned, t_hi, t_lo = sem("turned"), sem("t_hi"), sem("t_lo")
        pv = sem("pv")
        u_hi_ready, u_ready = sem("u_hi_ready"), sem("u_ready")
        mask_loaded, bias_ready = sem("mask_loaded"), sem("bias_ready")
        y_loaded, y_stored = sem("y_loaded"), sem("y_stored")

        passed_dve, passed_pool = sem("passed_dve"), sem("passed_pool")

        def unit_before(i, s):
            while True:
                s -= 1
                if isinstance(i, int) and i + s // SLOTS < -1:
                    return None
                if s % SLOTS in UNITS:
                    kind, dn, m = UNITS[s % SLOTS]
                    if valid(i, dn + s // SLOTS):
                        return kind, dn + s // SLOTS, m

        def unit_to_evacuate(s):
            if (s - 1) % SLOTS not in UNITS:
                return None
            kind, dn, m = UNITS[(s - 1) % SLOTS]
            return kind, dn + (s - 1) // SLOTS, m

        block = ctx.enter_context(nc.Block())

        @block.sync
        def _(sp):
            def batch(n):
                return bass.ds(n // QUADS, 1) if not isinstance(n, int) else slice(n // QUADS, n // QUADS + 1)

            def quad(n):
                return bass.ds(n % QUADS, 1) if not isinstance(n, int) else slice(n % QUADS, n % QUADS + 1)

            def free_buffer(i, p):
                r, before = 0, p - RAW
                while True:
                    if before < 0:
                        r, before = r - 1, max(x for x in range(len(LOADS)) if x % RAW == p % RAW)
                    kind, dn, m = LOADS[before]
                    if isinstance(i, int) and i + r < -1:
                        return
                    if valid(i, dn + r):
                        wait(sp, split[kind], i, 2 * PIECES[kind], 2 * (PIECES[kind] * (dn + r) + m + 1))
                        return
                    before -= RAW

            def load(i, p):
                kind, dn, m = LOADS[p]
                if not valid(i, dn):
                    return
                free_buffer(i, p)
                n, dst = i + dn, raw[:, p % RAW]
                arrived = loaded[LOADS[p]]
                if kind == "wo":
                    src = wo[quad(n)].rearrange("o d h n -> d (o h n)")[:, m * 512:(m + 1) * 512]
                    sp.dma_start(dst[0:DH], src).then_inc(arrived, 16)
                    sp.dma_start(dst[DH:P], src).then_inc(arrived, 16)
                elif kind == "ctx":
                    sp.dma_start(dst, ctxT[batch(n), :, m].rearrange("o p k -> p (o k)")).then_inc(arrived, 16)
                elif kind == "xn":
                    sp.dma_start(dst, xnT[batch(n), :, m].rearrange("o p q -> p (o q)")).then_inc(arrived, 16)
                else:
                    w = {"wq": wq, "wk": wk, "wv": wv}[kind]
                    sp.dma_start(dst, w[quad(n)].rearrange("o p n -> p (o n)")).then_inc(arrived, 16)

            def body(i):
                load(i, 0)
                load(i, 1)
                if valid(i, -1):
                    wait(sp, y_stored, i, 16, -16)
                    sp.dma_start(y_sb[:], y[batch(i - 1)].rearrange("o p t d -> p (o t) d")).then_inc(y_loaded, 16)
                if valid(i, 1):
                    wait(sp, bias_ready, i, 2, 2)
                    sp.dma_start(mask_raw[:], mask[batch(i + 1), :].partition_broadcast(P)).then_inc(mask_loaded, 16)
                for p in range(2, len(LOADS)):
                    load(i, p)
                if valid(i, -1):
                    wait(sp, done["o"], i, 2, 0)
                    sp.dma_start(y[batch(i - 1)].rearrange("o p t d -> p (o t) d"), y_sb[:]).then_inc(y_stored, 16)

            run_loop(sp, body, -1, STEPS)
            sp.wait_ge(y_stored, 16 * STEPS)

        @block.gpsimd
        def _(pool):
            pool.memset(ident[:], 0.0).then_inc(ident0, 1)
            pool.wait_ge(ident0, 1)
            pool.affine_select(out=ident[:], in_=ident[:], compare_op=ALU.not_equal, fill=1.0, base=0,
                               pattern=[[-1, P]], channel_multiplier=1).then_inc(ident_ready, 1)

            def operands(job):
                kind, _, m = job
                if kind == "vs":
                    return v_raw[:, :, m], v_st[:, m, :, 0], v_st[:, m, :, 1]
                src = raw[:, LOADS.index(job) % RAW]
                if kind == "wo":
                    src = src.rearrange("p (h n) -> p h n", h=2)
                    return src, wo_hi[:, 2 * m:2 * m + 2], wo_lo[:, 2 * m:2 * m + 2]
                if kind == "ctx":
                    return src, ctx_hi[:, m], ctx_lo[:, m]
                if kind == "xn":
                    return src, xn_hi[:, m], xn_lo[:, m]
                if kind == "wq":
                    src = src.rearrange("p (h d) -> p h d", d=DH).unsqueeze(2).broadcast_to([P, DC * QUAD, 2, DH])
                    return (src, wq_hi[:].rearrange("p c h t d -> p (c h) t d"),
                            wq_lo[:].rearrange("p c h t d -> p (c h) t d"))
                hi, lo = (wk_hi, wk_lo) if kind == "wk" else (wv_hi, wv_lo)
                return src.rearrange("p (c n) -> p c n", c=DC), hi[:], lo[:]

            def before_split(i, kind, dn, m):
                if kind == "vs":
                    if m == 0:
                        wait(pool, done["v"], i, 4, 4 * dn + 4)
                    wait(pool, pv, i, 32, 32 * (dn - 1) + KC * (m + 1))
                    return
                wait(pool, loaded[kind, dn, m], i, 32 if kind == "wo" else 16, (32 if kind == "wo" else 16) * (dn + 1))
                if kind == "wo" and m == 0:
                    wait(pool, unit["o"], i, 2, 2 * dn)
                if kind == "wk" or (kind == "ctx" and m == 0):
                    wait(pool, unit["k"], i, 4, 4 * dn)
                if kind == "wq" or (kind == "xn" and m == 0):
                    wait(pool, unit["q"], i, 4, 4 * dn)
                if kind == "wv":
                    wait(pool, unit["v"], i, 4, 4 * dn)

            def body(i):
                for s in range(SLOTS):
                    jobs = [j for j in JOBS.get(s, []) if valid(i, j[1])]
                    for kind, dn, m in jobs:
                        before_split(i, kind, dn, m)
                        src, hi, lo = operands((kind, dn, m))
                        stand_alone(pool, passed_pool)
                        pool.tensor_scalar(hi, src, 1.0, 1.0, ALU.mult, ALU.mult).then_inc(split[kind], 1)
                    for kind, dn, m in jobs:
                        src, hi, lo = operands((kind, dn, m))
                        wait(pool, split[kind], i, 2 * PIECES[kind], 2 * (PIECES[kind] * dn + m) + 1)
                        pool.tensor_tensor(lo, src, hi.bitcast(F32), ALU.subtract).then_inc(split[kind], 1)
                    if s == 12 and valid(i, 1):
                        wait(pool, mask_loaded, i, 16, 32)
                        wait(pool, masked, i, SLOTS, 8)
                        stand_alone(pool, passed_pool)
                        pool.tensor_scalar(mask_bias[:, 0], mask_raw[:], -MASKED, MASKED, ALU.mult,
                                           ALU.add).then_inc(bias_ready, 1)
                    if s == 2 and valid(i, 0):
                        wait(pool, masked, i, SLOTS, 0)
                        stand_alone(pool, passed_pool)
                        pool.tensor_scalar(mask_bias[:, 1], mask_raw[:], -MASKED, MASKED, ALU.mult,
                                           ALU.add).then_inc(bias_ready, 1)
                    dn, g, j = at_lag(s, 1)
                    if valid(i, dn):
                        t = QT * g + j
                        wait(pool, inverted, i, SLOTS, SLOTS * dn + t + 1)
                        tile = probs[:, t % (2 * QT)]
                        stand_alone(pool, passed_pool)
                        pool.tensor_scalar(tile, tile, rinv[:, t:t + 1], 1.0, ALU.mult, ALU.mult).then_inc(normed, 1)

            run_loop(pool, body, -1, STEPS)

        @block.tensor
        def _(pe):
            def three(out, hi, lo, hi2, lo2, start, stop):
                pe.matmul(out, hi, hi2, start=start, stop=False)
                pe.matmul(out, hi, lo2, start=False, stop=False)
                return pe.matmul(out, lo, hi2, start=False, stop=stop)

            def project(kind, m):
                if kind == "k":
                    pair, h = m // 2, m % 2
                    cols = slice(pair * P, (pair + 1) * P)
                    for c in range(DC):
                        last = three(m_ps[:], wk_hi[:, c, cols], wk_lo[:, c, cols], ctx_hi[:, h * DC + c],
                                     ctx_lo[:, h * DC + c], c == 0, c == DC - 1)
                elif kind == "q":
                    for c in range(DC):
                        last = three(m_ps[:], wq_hi[:, c, m].rearrange("p t d -> p (t d)"),
                                     wq_lo[:, c, m].rearrange("p t d -> p (t d)"), xn_hi[:, c], xn_lo[:, c],
                                     c == 0, c == DC - 1)
                elif kind == "v":
                    for r in range(2):
                        kc = 2 * m + r
                        h, keys = kc // 4, slice(kc % 4 * P, (kc % 4 + 1) * P)
                        for c in range(DC):
                            last = three(m_ps[:, r * D:(r + 1) * D], ctx_hi[:, h * DC + c, keys],
                                         ctx_lo[:, h * DC + c, keys], wv_hi[:, c], wv_lo[:, c],
                                         c == 0, c == DC - 1)
                else:
                    for r in range(2):
                        qs = slice((2 * m + r) * P, (2 * m + r + 1) * P)
                        for g in range(QUAD):
                            last = three(m_ps[:, r * D:(r + 1) * D], u_hi[:, g, qs], u_lo[:, g, qs],
                                         wo_hi[:, g], wo_lo[:, g], g == 0, g == QUAD - 1)
                return last

            def transpose_chunk(i, dn, g, j, r):
                c = KC * g + 2 * j + r
                wait(pe, t_lo, i, 32, 32 * dn + c - 1)
                if j == 0 and r == 0:
                    wait(pe, normed, i, SLOTS, SLOTS * dn + QT * (g + 1))
                for t in range(QT):
                    last = pe.transpose(t_ps[:, r, t * P:(t + 1) * P],
                                        probs[:, (QT * g + t) % (2 * QT), (2 * j + r) * P:(2 * j + r + 1) * P],
                                        ident[:])
                last.then_inc(turned, 1)

            def score(i, s):
                g, j = s // QT, s % QT
                wait(pe, exped, i, SLOTS, s - 1)
                if j == 0:
                    wait(pe, done["q"], i, 4, g + 1)
                    if g % 2 == 0:
                        wait(pe, done["k"], i, 4, g + 2)
                qs = slice(j * P, (j + 1) * P)
                for part in (q_hi, q_lo):
                    for h in range(NH):
                        last = pe.matmul(s_ps[:, s % 2, h], part[:, g, qs], k_st[:, g, h * 512:(h + 1) * 512],
                                         start=part is q_hi, stop=part is q_lo)
                last.then_inc(scored, 1)

            def values(i, dn, g, j, turns):
                for r in range(2):
                    c = KC * g + 2 * j + r
                    if not turns:
                        wait(pe, t_lo, i, 32, 32 * dn + c + 1)
                    if j == 0 and r == 0:
                        wait(pe, u_ready, i, 4, 4 * dn + g)
                        wait(pe, split["vs"], i, 8, 2 * (4 * dn + g + 1))
                    lhsT = v_st[:, g, 2 * j + r].rearrange("p t d -> p (t d)")
                    pe.matmul(pv_ps[:], lhsT, pt_hi[:, c % 4], start=c % KC == 0, stop=False)
                    pe.matmul(pv_ps[:], lhsT, pt_lo[:, c % 4], start=False, stop=c % KC == KC - 1).then_inc(pv, 1)

            def ready(i, kind, dn, m):
                if kind == "k":
                    if m == 0:
                        wait(pe, split["wk"], i, 2, 2 * dn + 2)
                    if m < 2:
                        wait(pe, split["ctx"], i, 8, 8 * dn + 4 * (m + 1))
                elif kind == "q" and m == 0:
                    wait(pe, split["wq"], i, 2, 2 * dn + 2)
                    wait(pe, split["xn"], i, 4, 4 * dn + 4)
                elif kind == "v" and m == 0:
                    wait(pe, split["wv"], i, 2, 2 * dn + 2)
                elif kind == "o" and m == 0:
                    wait(pe, split["wo"], i, 4, 4 * dn + 4)
                    wait(pe, u_ready, i, 4, 4 * dn + 4)

            def body(i):
                for s in range(SLOTS):
                    dt, gt, jt = at_lag(s, T_LAG)
                    dv, gv, jv = at_lag(s, PV_LAG)
                    turns = valid(i, dt)
                    if turns:
                        transpose_chunk(i, dt, gt, jt, 0)
                    if valid(i, 0):
                        score(i, s)
                    if turns:
                        transpose_chunk(i, dt, gt, jt, 1)
                    if valid(i, dv):
                        values(i, dv, gv, jv, turns)
                    if s in UNITS and valid(i, UNITS[s][1]):
                        kind, dn, m = UNITS[s]
                        before = unit_before(i, s)
                        if before:
                            pk, pd, pm = before
                            wait(pe, done[pk], i, PER_QUAD[pk], PER_QUAD[pk] * pd + pm + 1)
                        ready(i, kind, dn, m)
                        project(kind, m).then_inc(unit[kind], 1)

            pe.wait_ge(ident_ready, 1)
            run_loop(pe, body, -1, STEPS)

        @block.scalar
        def _(act):
            def evacuate(i, kind, dn, m):
                if kind == "o":
                    return
                n = PER_QUAD[kind] * dn + m
                wait(act, unit[kind], i, PER_QUAD[kind], n + 1)
                if kind == "k":
                    keys = slice(m % 2 * 512, (m % 2 + 1) * 512)
                    a = 2 * (m // 2)
                    act.activation(k_st[0:DH, a, keys], m_ps[0:DH], ACT.Copy).then_inc(unit_hi["k"], 1)
                    act.activation(k_st[DH:P, a + 1, keys], m_ps[DH:P], ACT.Copy).then_inc(unit_hi["k"], 1)
                elif kind == "q":
                    act.activation(q_hi[:, m], m_ps[:], ACT.Copy, scale=-DH ** -0.5).then_inc(unit_hi["q"], 1)
                else:
                    if m == 0:
                        wait(act, split["vs"], i, 8, 8 * dn)
                    act.activation(v_raw[:, 2 * m:2 * m + 2].rearrange("p c h d -> p c (h d)"),
                                   m_ps[:].rearrange("p (c n) -> p c n", c=2), ACT.Copy).then_inc(done["v"], 1)

            def chunk_hi(i, dn, g, j, r):
                c = KC * g + 2 * j + r
                wait(act, turned, i, 32, 32 * dn + c + 1)
                wait(act, pv, i, 32, 32 * dn + c - 3)
                act.activation(pt_hi[:, c % 4], t_ps[:, r], ACT.Copy).then_inc(t_hi, 1)

            def body(i):
                for s in range(SLOTS):
                    du, gu, ju = at_lag(s, U_LAG)
                    if ju == QT - 1 and valid(i, du):
                        wait(act, pv, i, 32, 32 * du + KC * (gu + 1))
                        if gu == 0:
                            wait(act, unit["o"], i, 2, 2 * du)
                        act.activation(u_hi[:, gu], pv_ps[:], ACT.Copy).then_inc(u_hi_ready, 1)
                    todo = unit_to_evacuate(s)
                    if todo and valid(i, todo[1]):
                        evacuate(i, *todo)
                    dt, gt, jt = at_lag(s, T_LAG)
                    if valid(i, dt):
                        chunk_hi(i, dt, gt, jt, 0)
                    de, ge, je = at_lag(s, 1)
                    if valid(i, de):
                        t = QT * ge + je
                        wait(act, masked, i, SLOTS, SLOTS * de + t + 1)
                        if je == 0:
                            wait(act, turned, i, 32, 32 * de + KC * (ge - 1))
                        act.activation(probs[:, t % (2 * QT)], s_ps[:, t % 2], ACT.Exp, bias=low[:, t:t + 1],
                                       scale=-1.0, accum_out=rowsum[:, t:t + 1]).then_inc(exped, 1)
                    if valid(i, dt):
                        chunk_hi(i, dt, gt, jt, 1)

            run_loop(act, body, -1, STEPS)

        @block.vector
        def _(dve):
            def evacuate(i, kind, dn, m):
                n = PER_QUAD[kind] * dn + m
                if kind == "k":
                    keys = slice(m % 2 * 512, (m % 2 + 1) * 512)
                    a = 2 * (m // 2)
                    wait(dve, unit_hi["k"], i, 8, 2 * n + 1)
                    dve.tensor_tensor(k_st[DH:P, a, keys], m_ps[0:DH], k_st[0:DH, a, keys].bitcast(F32),
                                      ALU.subtract).then_inc(k_lo_a, 1)
                    wait(dve, unit_hi["k"], i, 8, 2 * n + 2)
                    wait(dve, k_lo_a, i, 4, n + 1)
                    dve.tensor_tensor(k_st[0:DH, a + 1, keys], m_ps[DH:P], k_st[DH:P, a + 1, keys].bitcast(F32),
                                      ALU.subtract).then_inc(done["k"], 1)
                elif kind == "q":
                    wait(dve, unit_hi["q"], i, 4, n + 1)
                    dve.scalar_tensor_tensor(q_lo[:, m], m_ps[:], -DH ** -0.5, q_hi[:, m].bitcast(F32),
                                             ALU.mult, ALU.subtract).then_inc(done["q"], 1)
                elif kind == "o":
                    wait(dve, unit["o"], i, 2, n + 1)
                    if m == 0:
                        wait(dve, y_loaded, i, 16, 16 * (dn + 1))
                    dst = y_sb[:, 2 * m:2 * m + 2].rearrange("p t d -> p (t d)")
                    dve.tensor_tensor(dst, m_ps[:], dst, ALU.add).then_inc(done["o"], 1)

            def chunk_lo(i, dn, g, j, r):
                c = KC * g + 2 * j + r
                wait(dve, t_hi, i, 32, 32 * dn + c + 1)
                dve.tensor_tensor(pt_lo[:, c % 4], t_ps[:, r], pt_hi[:, c % 4].bitcast(F32),
                                  ALU.subtract).then_inc(t_lo, 1)

            def body(i):
                for s in range(SLOTS):
                    du, gu, ju = at_lag(s, U_LAG)
                    if ju == QT - 1 and valid(i, du):
                        wait(dve, u_hi_ready, i, 4, 4 * du + gu + 1)
                        dve.tensor_tensor(u_lo[:, gu], pv_ps[:], u_hi[:, gu].bitcast(F32),
                                          ALU.subtract).then_inc(u_ready, 1)
                    todo = unit_to_evacuate(s)
                    if todo and valid(i, todo[1]):
                        evacuate(i, *todo)
                    dt, gt, jt = at_lag(s, T_LAG)
                    if valid(i, dt):
                        chunk_lo(i, dt, gt, jt, 0)
                    if valid(i, 0):
                        wait(dve, scored, i, SLOTS, s + 1)
                        if s == 0:
                            wait(dve, bias_ready, i, 2, 1)
                        if s == 8:
                            wait(dve, bias_ready, i, 2, 2)
                        stand_alone(dve, passed_dve)
                        tile = s_ps[:, s % 2]
                        bias = mask_bias[:, s // 8].rearrange("p (h k) -> p h k", h=NH)
                        dve.tensor_tensor_reduce(out=tile, in0=tile, in1=bias, scale=1.0, scalar=LARGEST,
                                                 op0=ALU.add, op1=ALU.min,
                                                 accum_out=low[:, s:s + 1]).then_inc(masked, 1)
                    de, ge, je = at_lag(s, 1)
                    if valid(i, de):
                        t = QT * ge + je
                        wait(dve, exped, i, SLOTS, SLOTS * de + t + 1)
                        dve.reciprocal(rinv[:, t:t + 1], rowsum[:, t:t + 1]).then_inc(inverted, 1)
                    if valid(i, dt):
                        chunk_lo(i, dt, gt, jt, 1)

            run_loop(dve, body, -1, STEPS)


TILES = 2 * QT
PAIRS = B // 2
STATS_LAG, TURN_LAG, SPLIT_LAG, DOWN_LAG, OUT_LAG = 1, 2, 3, 4, 5


def feedforward_stage(nc, w1T, w2T, g1, n1, b1, g2, n2, b2, y, out):
    with ExitStack() as ctx:
        sb = lambda name, shape, dt=F32: ctx.enter_context(nc.sbuf_tensor(name, shape, dt))
        sem = lambda name: ctx.enter_context(nc.semaphore(name))
        w1_raw, w2_raw = sb("w1_raw", [P, DC * HID]), sb("w2_raw", [P, HC * D])
        above, below = sb("above", [P, HC * D]), sb("below", [P, HC * D])
        t1, t2 = sb("t1", [P, DC, HID], F32R), sb("t2", [P, HC, D], F32R)
        abs_part, w_scale, w_mean = sb("abs_part", [P, 2]), sb("w_scale", [P, 2]), sb("w_mean", [P, 2])
        ones, ident, half = sb("ones_f", [P, P]), sb("ident_f", [P, P]), sb("half_f", [P, QT])
        g1_sb, n1_sb = sb("g1_sb", [P, DC]), sb("n1_sb", [P, DC])
        g2_sb, n2_sb = sb("g2_sb", [P, HC]), sb("n2_sb", [P, HC])
        b1_sb, b2_sb = sb("b1_sb", [P, HID]), sb("b2_sb", [P, D])
        y_in, yb = sb("y_in", [P, 2, QT, D]), sb("yb", [P, 2, QT, D])
        z, hn = sb("z", [P, QT, D]), sb("hn", [P, QT, D])
        ht, ht_hi, ht_lo = sb("ht", [P, DC, NQ]), sb("ht_hi", [P, 2, DC, NQ], F32R), sb("ht_lo", [P, 2, DC, NQ], F32R)
        fstats, fmv = sb("fstats", [P, QT, 6]), sb("fmv", [P, 2, QT, 2])
        fvar, frstd = sb("fvar", [P, 2, QT]), sb("frstd", [P, 2, QT])
        pre, act_out = sb("pre", [P, 2, HID]), sb("act_out", [P, 2, HID])
        gn, gt = sb("gn", [P, 2, HID]), sb("gt", [P, 2, HC, P])
        gt_hi, gt_lo = sb("gt_hi", [P, 2, HC, P], F32R), sb("gt_lo", [P, 2, HC, P], F32R)
        gstats, gmv = sb("gstats", [P, 2, 2, 6]), sb("gmv", [P, 2, 2])
        gvar, grstd, gbias = sb("gvar", [P, 2]), sb("grstd", [P, 2]), sb("gbias", [P, 2])
        out_sb = sb("out_sb", [P, 2, QT, D])
        f_ps = ctx.enter_context(nc.psum_tensor("f_ps", [P, 2, HID], F32))
        g_ps = ctx.enter_context(nc.psum_tensor("g_ps", [P, HC, P], F32))
        h_ps = ctx.enter_context(nc.psum_tensor("h_ps", [P, 512], F32))
        o_ps = ctx.enter_context(nc.psum_tensor("o_ps", [P, 512], F32))

        w_in, vec_in, y_in_s = sem("w_in"), sem("vec_in"), [sem("y_in_s0"), sem("y_in_s1")]
        ident0, const, absed, summed = sem("f_ident0"), sem("f_const"), sem("absed"), sem("summed")
        prep, ternary = sem("prep"), sem("ternary")
        fstat, faggr, fvared, frstded = sem("fstat"), sem("faggr"), sem("fvared"), sem("frstded")
        z_ready, hn_ready, yb_ready = sem("z_ready"), sem("hn_ready"), sem("yb_ready")
        h_turned, h_taken, h_hi, h_lo = sem("h_turned"), sem("h_taken"), sem("h_hi"), sem("h_lo")
        up, pre_ready, gelued = sem("up"), sem("pre_ready"), sem("gelued")
        gstat, gaggr, gvared, grstded, gbiased = (sem(x) for x in ("gstat", "gaggr", "gvared", "grstded", "gbiased"))
        gn_ready, g_turned, gt_ready, g_hi, g_lo = (sem(x) for x in ("gn_ready", "g_turned", "gt_ready", "g_hi", "g_lo"))
        down, out_ready, out_stored = sem("down"), sem("out_ready"), [sem("out_stored0"), sem("out_stored1")]

        passed = sem("f_passed")

        def tile_ok(i, s, lag):
            return not isinstance(i, int) or 0 <= TILES * i + s - lag < B * QT

        def front_ok(i, s):
            return not isinstance(i, int) or 0 <= 2 * i + s // QT + 1 < B

        def loop(eng, body):
            body(-1)
            body(0)
            with eng.Fori(1, PAIRS - 1) as i:
                body(i)
            body(PAIRS - 1)
            body(PAIRS)

        block = ctx.enter_context(nc.Block())

        @block.sync
        def _(sp):
            sp.dma_start(w1_raw[:], w1T).then_inc(w_in, 16)
            sp.dma_start(w2_raw[:], w2T).then_inc(w_in, 16)
            for dst, src in ((g1_sb, g1), (n1_sb, n1), (g2_sb, g2), (n2_sb, n2)):
                sp.dma_start(dst[:], src).then_inc(vec_in, 16)
            for dst, src in ((b1_sb, b1), (b2_sb, b2)):
                sp.dma_start(dst[:], src.unsqueeze(0).partition_broadcast(P)).then_inc(vec_in, 16)

            def body(i):
                for s in range(0, TILES, QT):
                    u = (s // QT + 1) % 2
                    n = s // QT + 1
                    if front_ok(i, s):
                        wait(sp, z_ready, i, 2, n - 1)
                        wait(sp, yb_ready, i, 2, n - 1)
                        b = 2 * i + n
                        src = y[b:b + 1] if isinstance(i, int) else y[bass.ds(b, 1)]
                        sp.dma_start(y_in[:, u], src.rearrange("o p t d -> p (o t) d")).then_inc(y_in_s[u], 16)
                    u = (s // QT + 1) % 2
                    if tile_ok(i, s, QT):
                        wait(sp, out_ready, i, TILES, s)
                        b = 2 * i + s // QT - 1
                        dst = out[b:b + 1] if isinstance(i, int) else out[bass.ds(b, 1)]
                        sp.dma_start(dst.rearrange("o (t p) d -> p (o t) d", p=P), out_sb[:, u])\
                            .then_inc(out_stored[u], 16)

            loop(sp, body)
            for u in range(2):
                sp.wait_ge(out_stored[u], 16 * PAIRS)

        @block.gpsimd
        def _(pool):
            pool.memset(half[:], -0.5).then_inc(const, 1)
            pool.memset(ones[:], 1.0).then_inc(const, 1)
            pool.memset(ident[:], 0.0).then_inc(ident0, 1)
            pool.wait_ge(ident0, 1)
            pool.affine_select(out=ident[:], in_=ident[:], compare_op=ALU.not_equal, fill=1.0, base=0,
                               pattern=[[-1, P]], channel_multiplier=1).then_inc(const, 1)
            pool.wait_ge(const, 3)
            pool.wait_ge(vec_in, 96)

            def body(i):
                for s in range(TILES):
                    u, n = (s // QT + 1) % 2, s // QT + 1
                    if tile_ok(i, s, STATS_LAG):
                        r = (s - STATS_LAG) % 2
                        wait(pool, gvared, i, TILES, s - STATS_LAG + 1)
                        pool.tensor_tensor(grstd[:, r:r + 1], gvar[:, r:r + 1], half[:, 0:1],
                                           ALU.pow).then_inc(grstded, 1)
                    if front_ok(i, s):
                        if s % QT == 0 or s % QT == 1:
                            e = s % QT
                            wait(pool, fvared, i, 4, 2 * n + e + 1)
                            pool.tensor_tensor(frstd[:, e], fvar[:, e], half[:], ALU.pow).then_inc(frstded, 1)
                    if s % QT == 1 and tile_ok(i, s, 1):
                        v = s // QT
                        wait(pool, y_in_s[v], i, 16, 16)
                        wait(pool, out_ready, i, TILES, QT * (v - 1))
                        for t in range(QT):
                            last = pool.tensor_tensor(yb[:, v, t], y_in[:, v, t], b2_sb[:], ALU.add)
                        last.then_inc(yb_ready, 1)
                    if tile_ok(i, s, SPLIT_LAG):
                        r = (s - SPLIT_LAG) % 2
                        wait(pool, g_hi, i, TILES, s - SPLIT_LAG + 1)
                        pool.tensor_tensor(gt_lo[:, r], gt[:, r], gt_hi[:, r].bitcast(F32), ALU.subtract)\
                            .then_inc(g_lo, 1)
                    if front_ok(i, s) and s % QT == QT - 1:
                        for c in range(DC):
                            wait(pool, h_hi, i, 4, 2 * n + c + 1)
                            pool.tensor_tensor(ht_lo[:, u, c], ht[:, c], ht_hi[:, u, c].bitcast(F32),
                                               ALU.subtract).then_inc(h_lo, 1)

            loop(pool, body)

        @block.tensor
        def _(pe):
            pe.wait_ge(const, 3)
            for w in range(2):
                pe.wait_ge(absed, w + 1)
                pe.matmul(h_ps[:, w:w + 1], ones[:], abs_part[:, w:w + 1], start=True, stop=True).then_inc(summed, 1)
            pe.wait_ge(ternary, 2)

            def turn_h(i, s, c):
                u, n = (s // QT + 1) % 2, s // QT + 1
                wait(pe, hn_ready, i, 2, n + 1)
                wait(pe, h_taken, i, 4, 2 * n + c)
                for t in range(QT):
                    last = pe.transpose(h_ps[:, t * P:(t + 1) * P], hn[:, t, c * P:(c + 1) * P], ident[:])
                last.then_inc(h_turned, 1)

            def body(i):
                for s in range(TILES):
                    u = s // QT % 2
                    if front_ok(i, s) and s % QT == QT - 1:
                        turn_h(i, s, 0)
                    if tile_ok(i, s, TURN_LAG):
                        r = (s - TURN_LAG) % 2
                        wait(pe, gn_ready, i, TILES, s - TURN_LAG + 1)
                        wait(pe, gt_ready, i, TILES, s - TURN_LAG)
                        for c in range(HC):
                            last = pe.transpose(g_ps[:, c], gn[:, r, c * P:(c + 1) * P], ident[:])
                        last.then_inc(g_turned, 1)
                    if tile_ok(i, s, 0):
                        if s % QT == 0:
                            wait(pe, h_lo, i, 4, 2 * (s // QT) + 2)
                        wait(pe, pre_ready, i, TILES, s - 1)
                        rows = slice(s % QT * P, (s % QT + 1) * P)
                        for c in range(DC):
                            for part in (ht_hi, ht_lo):
                                for h in range(2):
                                    last = pe.matmul(f_ps[:, s % 2, h * 512:(h + 1) * 512], part[:, u, c, rows],
                                                     t1[:, c, h * 512:(h + 1) * 512],
                                                     start=c == 0 and part is ht_hi, stop=c == DC - 1 and part is ht_lo)
                        last.then_inc(up, 1)
                    if tile_ok(i, s, DOWN_LAG):
                        r = (s - DOWN_LAG) % 2
                        wait(pe, g_lo, i, TILES, s - DOWN_LAG + 1)
                        wait(pe, out_ready, i, TILES, s - DOWN_LAG)
                        for c in range(HC):
                            pe.matmul(o_ps[:, 0:D], gt_hi[:, r, c], t2[:, c], start=c == 0, stop=False)
                            last = pe.matmul(o_ps[:, 0:D], gt_lo[:, r, c], t2[:, c], start=False, stop=c == HC - 1)
                        last.then_inc(down, 1)
                    if front_ok(i, s) and s % QT == QT - 1:
                        turn_h(i, s, 1)

            loop(pe, body)

        @block.scalar
        def _(act):
            act.wait_ge(w_in, 32)
            act.activation(above[:], w1_raw[:], ACT.Abs, accum_out=abs_part[:, 0:1]).then_inc(absed, 1)
            act.activation(below[:], w2_raw[:], ACT.Abs, accum_out=abs_part[:, 1:2]).then_inc(absed, 1)
            act.wait_ge(vec_in, 96)

            def body(i):
                for s in range(TILES):
                    if tile_ok(i, s, STATS_LAG):
                        r = (s - STATS_LAG) % 2
                        wait(act, gbiased, i, TILES, s - STATS_LAG + 1)
                        wait(act, g_turned, i, TILES, s - STATS_LAG - 1)
                        act.activation(gn[:, r], act_out[:, r], ACT.Identity, bias=gbias[:, r:r + 1],
                                       scale=grstd[:, r:r + 1]).then_inc(gn_ready, 1)
                    if tile_ok(i, s, TURN_LAG):
                        r = (s - TURN_LAG) % 2
                        wait(act, g_turned, i, TILES, s - TURN_LAG + 1)
                        wait(act, g_lo, i, TILES, s - TURN_LAG - 1)
                        for c in range(HC):
                            last = act.activation(gt[:, r, c], g_ps[:, c], ACT.Identity, bias=n2_sb[:, c:c + 1],
                                                  scale=g2_sb[:, c:c + 1])
                        last.then_inc(gt_ready, 1)
                    if tile_ok(i, s, 0):
                        wait(act, pre_ready, i, TILES, s + 1)
                        act.activation(act_out[:, s % 2], pre[:, s % 2], ACT.Gelu).then_inc(gelued, 1)
                    if front_ok(i, s) and s % QT == QT - 1:
                        n = s // QT + 1
                        for c in range(DC):
                            wait(act, h_turned, i, 4, 2 * n + c + 1)
                            wait(act, h_lo, i, 4, 2 * n + c - 1)
                            act.activation(ht[:, c], h_ps[:], ACT.Identity, bias=n1_sb[:, c:c + 1],
                                           scale=g1_sb[:, c:c + 1]).then_inc(h_taken, 1)

            loop(act, body)

        @block.vector
        def _(dve):
            steps = [0]

            def then(ins):
                ins.then_inc(prep, 1)
                steps[0] += 1
                dve.wait_ge(prep, steps[0])

            dve.wait_ge(summed, 2)
            then(dve.tensor_scalar(w_mean[:], h_ps[:, 0:2], 1.0 / (HID * D), 1e-5, ALU.mult, ALU.max))
            then(dve.reciprocal(w_scale[:], w_mean[:]))
            then(dve.reciprocal(w_mean[:], w_scale[:]))
            for w, (src, t) in enumerate(((w1_raw, t1), (w2_raw, t2))):
                scale = w_scale[:, w:w + 1]
                then(dve.tensor_scalar(above[:], src[:], scale, 0.5, ALU.mult, ALU.is_gt))
                then(dve.tensor_scalar(below[:], src[:], scale, -0.5, ALU.mult, ALU.is_lt))
                dve.tensor_tensor(t[:].rearrange("p c n -> p (c n)"), above[:], below[:], ALU.subtract)\
                    .then_inc(ternary, 1)
                dve.wait_ge(ternary, w + 1)
            dve.wait_ge(vec_in, 96)

            def statistics(i, rows, e, n):
                for t in range(QT):
                    last = dve.bn_stats(fstats[:, t], rows[:, t])
                last.then_inc(fstat, 1)
                wait(dve, fstat, i, 4, 2 * n + e + 1)
                stand_alone(dve, passed)
                for t in range(QT):
                    last = dve.bn_aggr(fmv[:, e, t], fstats[:, t])
                last.then_inc(faggr, 1)
                wait(dve, faggr, i, 4, 2 * n + e + 1)
                dve.tensor_scalar(fvar[:, e], fmv[:, e, :, 1], EPS, None, ALU.add).then_inc(fvared, 1)

            def normalize(dst, rows, e):
                for t in range(QT):
                    last = dve.tensor_scalar(dst[:, t], rows[:, t], fmv[:, e, t, 0:1], frstd[:, e, t:t + 1],
                                             ALU.subtract, ALU.mult)
                return last

            def front(i, s):
                u, n = (s // QT + 1) % 2, s // QT + 1
                if s % QT == 0:
                    wait(dve, y_in_s[u], i, 16, 16 * (n // 2 + 1))
                    statistics(i, y_in[:, u], 0, n)
                elif s % QT == 1:
                    wait(dve, frstded, i, 4, 2 * n + 1)
                    normalize(z, y_in[:, u], 0).then_inc(z_ready, 1)
                    wait(dve, z_ready, i, 2, n + 1)
                    statistics(i, z, 1, n)
                elif s % QT == 2:
                    wait(dve, frstded, i, 4, 2 * n + 2)
                    wait(dve, h_turned, i, 4, 2 * n)
                    normalize(hn, z, 1).then_inc(hn_ready, 1)
                else:
                    for c in range(DC):
                        wait(dve, h_taken, i, 4, 2 * n + c + 1)
                        wait(dve, up, i, TILES, QT * (n - 1))
                        dve.tensor_copy(ht_hi[:, u, c], ht[:, c]).then_inc(h_hi, 1)

            def body(i):
                for s in range(TILES):
                    if tile_ok(i, s, OUT_LAG):
                        x = (s - OUT_LAG) % TILES
                        u, t = x // QT % 2, x % QT
                        wait(dve, down, i, TILES, s - OUT_LAG + 1)
                        if t == 0:
                            b = (s - OUT_LAG) // QT
                            wait(dve, out_stored[u], i, 16, 16 * (b // 2))
                            wait(dve, yb_ready, i, 2, b + 1)
                        dve.scalar_tensor_tensor(out_sb[:, u, t], o_ps[:, 0:D], w_mean[:, 1:2], yb[:, u, t],
                                                 ALU.mult, ALU.add).then_inc(out_ready, 1)
                    if tile_ok(i, s, SPLIT_LAG):
                        r = (s - SPLIT_LAG) % 2
                        wait(dve, gt_ready, i, TILES, s - SPLIT_LAG + 1)
                        wait(dve, down, i, TILES, s - SPLIT_LAG - 1)
                        dve.tensor_copy(gt_hi[:, r], gt[:, r]).then_inc(g_hi, 1)
                    if tile_ok(i, s, STATS_LAG):
                        r = (s - STATS_LAG) % 2
                        k = s - STATS_LAG + 1
                        wait(dve, gelued, i, TILES, k)
                        for h in range(2):
                            last = dve.bn_stats(gstats[:, r, h], act_out[:, r, h * 512:(h + 1) * 512])
                        last.then_inc(gstat, 1)
                        wait(dve, gstat, i, TILES, k)
                        stand_alone(dve, passed)
                        dve.bn_aggr(gmv[:, r], gstats[:, r]).then_inc(gaggr, 1)
                        wait(dve, gaggr, i, TILES, k)
                        dve.tensor_scalar(gvar[:, r:r + 1], gmv[:, r, 1:2], EPS, None, ALU.add).then_inc(gvared, 1)
                    if tile_ok(i, s, 0):
                        wait(dve, up, i, TILES, s + 1)
                        wait(dve, gelued, i, TILES, s - 1)
                        dve.scalar_tensor_tensor(pre[:, s % 2], f_ps[:, s % 2], w_mean[:, 0:1], b1_sb[:],
                                                 ALU.mult, ALU.add).then_inc(pre_ready, 1)
                    if tile_ok(i, s, STATS_LAG):
                        wait(dve, grstded, i, TILES, k)
                        dve.scalar_tensor_tensor(gbias[:, r:r + 1], gmv[:, r, 0:1], -1.0, grstd[:, r:r + 1],
                                                 ALU.mult, ALU.mult).then_inc(gbiased, 1)
                    if front_ok(i, s):
                        front(i, s)

            loop(dve, body)


def build(nc, x, ctxT, mask, wq, wk, wv, wo, b_out, g1, n1, w1T, b1, g2, n2, w2T, b2, out):
    xnT = nc.dram_tensor("xn_scratch", (B, P, DC, NQ), F32, kind="Internal").ap()
    y = nc.dram_tensor("y_scratch", (B, P, QT, D), F32, kind="Internal").ap()
    normalize_stage(nc, x, b_out, xnT, y)
    attention_stage(nc, ctxT, mask, wq, wk, wv, wo, xnT, y)
    feedforward_stage(nc, w1T, w2T, g1, n1, b1, g2, n2, b2, y, out)


def lay_out(inputs):
    import numpy as np

    get = {k: np.asarray(v) for k, v in inputs.items()}
    inner = HEADS * DH
    cols = QUAD * DH

    def quads(w):
        return np.ascontiguousarray(w.reshape(QUADS, cols, DC, P).transpose(0, 3, 2, 1)).reshape(QUADS, P, DC * cols)

    wkv = get["L0_xattn_Wkv"]
    return {
        "x": get["x"],
        "ctxT": np.ascontiguousarray(get["ctx_1024"].reshape(B, NH, 512, DC, P).transpose(0, 4, 1, 3, 2))
                  .reshape(B, P, NH * DC, 512),
        "mask": get["mask_BxS2_bf1"],
        "wq": quads(get["L0_xattn_Wq"]),
        "wk": quads(wkv[:inner]),
        "wv": quads(wkv[inner:]),
        "wo": np.ascontiguousarray(get["L0_xattn_Wout"].reshape(D, QUADS, QUAD, DH).transpose(1, 3, 2, 0)),
        "b_out": get["L0_xattn_b_out"],
        "g1": np.ascontiguousarray(get["L0_ffn_ln1_g"].reshape(DC, P).T),
        "n1": np.ascontiguousarray(get["L0_ffn_ln1_b"].reshape(DC, P).T),
        "w1T": np.ascontiguousarray(get["L0_ffn_w1"].reshape(HID, DC, P).transpose(2, 1, 0)).reshape(P, DC * HID),
        "b1": get["L0_ffn_b1"],
        "g2": np.ascontiguousarray(get["L0_ffn_ln2_g"].reshape(HC, P).T),
        "n2": np.ascontiguousarray(get["L0_ffn_ln2_b"].reshape(HC, P).T),
        "w2T": np.ascontiguousarray(get["L0_ffn_w2"].reshape(D, HC, P).transpose(2, 1, 0)).reshape(P, HC * D),
        "b2": get["L0_ffn_b2"],
    }


def kernel(**inputs):
    import numpy as np
    import concourse.bacc as bacc
    from concourse.bass_utils import run_bass_kernel_spmd

    nc = bacc.Bacc("TRN2", target_bir_lowering=False, num_devices=1)
    arrays, args = {}, []
    for name, a in lay_out(inputs).items():
        a = np.ascontiguousarray(a)
        arrays[f"in_{name}"] = a
        args.append(nc.dram_tensor(f"in_{name}", a.shape, mybir.dt.from_np(a.dtype), kind="ExternalInput").ap())
    args.append(nc.dram_tensor("out", (B, NQ, D), F32, kind="ExternalOutput").ap())
    build(nc, *args)
    r = run_bass_kernel_spmd(nc, [arrays], core_ids=[0])
    return r.results[0]["out"]
```

```python
from contextlib import ExitStack

import concourse.bass as bass
from concourse import mybir

ALU = mybir.AluOpType
ACT = mybir.ActivationFunctionType
AXES = mybir.AxisListType
F32 = mybir.dt.float32
F32R = mybir.dt.float32r
BF16 = mybir.dt.bfloat16
U8 = mybir.dt.uint8

P = 128
B, NQ, NKV, D = 8, 512, 1024, 256
HEADS, DH = 16, 64
QT = NQ // P
DC = D // P
QUAD = 4
PAIR = QUAD // 2
QUADS = HEADS // QUAD
STEPS = B * QUADS
SLOTS = QUAD * QT
KC = NKV // P
NH = NKV // 512
HID = 1024
HC = HID // P
EPS = 1e-5
MASKED = 3e38
LARGEST = 3.4e38
T_LAG, PV_LAG, U_LAG = 6, 7, 8

UNITS = {0: ("q", 0, 1), 1: ("v", 0, 2), 2: ("v", 0, 3), 3: ("k", 0, 2), 4: ("k", 0, 3), 7: ("q", 1, 0),
         10: ("o", -1, 0), 11: ("o", -1, 1), 12: ("k", 1, 0), 13: ("k", 1, 1), 14: ("v", 1, 0), 15: ("v", 1, 1)}
PER_QUAD = {"k": 4, "q": 2, "v": 4, "o": 2}
JOBS = {0: [("us", -1, 0)], 1: [("wq", 1, 0)], 2: [("xn", 1, 0)], 3: [("xn", 1, 1)], 4: [("vs", 0, 0)],
        5: [("vs", 0, 1)], 6: [("wk", 1, 0)], 7: [("ctx", 1, 0)], 8: [("us", -1, 1)], 9: [("ctx", 1, 1)],
        10: [("ctx", 1, 2)], 11: [("ctx", 1, 3)], 12: [("wv", 1, 0)], 13: [("vs", 0, 2)], 14: [("vs", 0, 3)],
        15: [("wo", 0, 0)]}
PIECES = {"wo": 1, "wk": 1, "ctx": 4, "wq": 1, "xn": 2, "wv": 1, "vs": 4, "us": 2}
LOADS = [j for s in range(SLOTS) for j in JOBS.get(s, []) if j[0] not in ("vs", "us")]
RAW = 4


def valid(i, dn):
    return not isinstance(i, int) or 0 <= i + dn < STEPS


def wait(eng, sem, i, per, off):
    if isinstance(i, int) and per * i + off <= 0:
        return
    assert isinstance(i, int) or per + off > 0
    eng.wait_ge(sem, per * i + off)


def stand_alone(eng, passed):
    eng.sem_inc(passed, 1)


def at_lag(s, lag):
    x = (s - lag) % SLOTS
    return (s - lag) // SLOTS, x // QT, x % QT


def run_loop(eng, body, first, last):
    for i in range(first, 1):
        body(i)
    with eng.Fori(1, STEPS - 1) as i:
        body(i)
    for i in range(STEPS - 1, last + 1):
        body(i)


RING = 4


class Weights:

    def __init__(self, sb):
        self.t1, self.t2 = sb("t1", [P, DC, HID], F32R), sb("t2", [P, HC, D], F32R)
        self.scale = sb("w_mean", [P, 2])
        self.b1_parts, self.two_ones = sb("b1_parts", [2, HID], F32R), sb("two_ones", [2, P], F32R)
        self.shift_row = sb("shift_row", [P, D])


def normalize_stage(nc, x, b_out, w1T, w2T, b1, n2, b2, weights, xnT, y):
    with ExitStack() as ctx:
        sb = lambda name, shape, dt=F32: ctx.enter_context(nc.sbuf_tensor(name, shape, dt))
        sem = lambda name: ctx.enter_context(nc.semaphore(name))
        rows = sb("n_rows", [P, RING, QT, D])
        xn = sb("n_xn", [P, 2, QT, D])
        yrow = sb("n_y", [P, 2, QT, D])
        xnt = sb("n_xnt", [P, 2, DC, NQ])
        bout, b2_row = sb("n_bout", [P, D]), sb("b2_row", [P, D])
        ident, ones = sb("n_ident", [P, P]), sb("n_ones", [P, P])
        half = sb("n_half", [P, QT])
        stats = sb("n_stats", [P, 2, QT, 6])
        mv = sb("n_mv", [P, 2, QT, 2])
        var = sb("n_var", [P, 2, QT])
        rstd = sb("n_rstd", [P, 2, QT])
        w1_raw, w2_raw = sb("w1_raw", [P, DC * HID]), sb("w2_raw", [P, HC * D])
        above, below = sb("above", [P, HC * D]), sb("below", [P, HC * D])
        abs_part, w_scale, w_mean = sb("abs_part", [P, 2]), sb("w_scale", [P, 2]), weights.scale
        n2_sb, n2_cols = sb("n2_sb", [P, HC]), sb("n2_cols", [P, HC, P])
        b1_raw, b1_scaled, b1_hi = sb("b1_raw", [2, HID]), sb("b1_scaled", [2, HID]), sb("b1_hi", [2, HID], F32R)
        b1_parts = weights.b1_parts
        ps = ctx.enter_context(nc.psum_tensor("n_ps", [P, 2, DC, NQ], F32))
        sum_ps = ctx.enter_context(nc.psum_tensor("sum_ps", [P, 512], F32))
        n2_ps = ctx.enter_context(nc.psum_tensor("n2_ps", [P, 512], F32))
        loaded = [sem(f"n_loaded{r}") for r in range(RING)]
        bias_in, const, ident0 = sem("n_bias_in"), sem("n_const"), sem("n_ident0")
        stat, aggr, vared, rstded = sem("n_stat"), sem("n_aggr"), sem("n_vared"), sem("n_rstd_s")
        normed, added, turned, copied = sem("n_normed"), sem("n_added"), sem("n_turned"), sem("n_copied")
        xn_stored, y_stored = [sem(f"n_xn_stored{v}") for v in range(2)], [sem(f"n_y_stored{v}") for v in range(2)]
        passed = sem("n_passed")
        w_in, vec_in, absed, summed = sem("w_in"), sem("vec_in"), sem("absed"), sem("summed")
        prep, ternary, n2_ready, shifted = sem("prep"), sem("ternary"), sem("n2_ready"), sem("shifted")
        ahead = {normed: RING, added: RING, turned: 2, copied: 2}
        stores = B // 2

        with nc.Block() as block:
            @block.sync
            def _(sp):
                for count, n in ahead.items():
                    sp.sem_inc(count, n)
                for v in range(2):
                    sp.sem_inc(xn_stored[v], 16)
                    sp.sem_inc(y_stored[v], 16)
                with sp.Fori(0, B // RING) as i:
                    for r in range(RING):
                        b = RING * i + r
                        sp.wait_ge(normed, b + 1)
                        sp.wait_ge(added, b + 1)
                        src = x[bass.ds(b, 1)].rearrange("o (t p) d -> p (o t) d", p=P)
                        sp.dma_start(rows[:, r], src).then_inc(loaded[r], 16)
                for v in range(2):
                    sp.wait_ge(xn_stored[v], 16 * (stores + 1))
                    sp.wait_ge(y_stored[v], 16 * (stores + 1))

            @block.gpsimd
            def _(pool):
                pool.dma_start(bout[:], b_out.unsqueeze(0).partition_broadcast(P)).then_inc(bias_in, 16)
                pool.memset(half[:], -0.5).then_inc(const, 1)
                pool.memset(ones[:], 1.0).then_inc(const, 1)
                pool.memset(ident[:], 0.0).then_inc(ident0, 1)
                pool.wait_ge(ident0, 1)
                pool.affine_select(out=ident[:], in_=ident[:], compare_op=ALU.not_equal, fill=1.0, base=0,
                                   pattern=[[-1, P]], channel_multiplier=1).then_inc(const, 1)
                pool.wait_ge(const, 2)
                pool.wait_ge(bias_in, 16)
                with pool.Fori(0, B // RING) as i:
                    for r in range(RING):
                        b, v = RING * i + r, r % 2
                        pool.wait_ge(vared, b + 1)
                        pool.tensor_tensor(rstd[:, v], var[:, v], half[:], ALU.pow).then_inc(rstded, 1)
                        pool.wait_ge(y_stored[v], 16 * (2 * i + r // 2) + 16)
                        for t in range(QT):
                            last = pool.tensor_tensor(yrow[:, v, t], rows[:, r, t], bout[:], ALU.add)
                        last.then_inc(added, 1)

            @block.vector
            def _(dve):
                with dve.Fori(0, B // RING) as i:
                    for r in range(RING):
                        b, v = RING * i + r, r % 2
                        dve.wait_ge(loaded[r], 16 * i + 16)
                        for t in range(QT):
                            last = dve.bn_stats(stats[:, v, t], rows[:, r, t])
                        last.then_inc(stat, 1)
                        dve.wait_ge(stat, b + 1)
                        stand_alone(dve, passed)
                        for t in range(QT):
                            last = dve.bn_aggr(mv[:, v, t], stats[:, v, t])
                        last.then_inc(aggr, 1)
                        dve.wait_ge(aggr, b + 1)
                        dve.tensor_scalar(var[:, v], mv[:, v, :, 1], EPS, None, ALU.add).then_inc(vared, 1)
                        dve.wait_ge(turned, b + 1)
                        dve.wait_ge(rstded, b + 1)
                        for t in range(QT):
                            last = dve.tensor_scalar(xn[:, v, t], rows[:, r, t], mv[:, v, t, 0:1],
                                                     rstd[:, v, t:t + 1], ALU.subtract, ALU.mult)
                        last.then_inc(normed, 1)

                steps = [0]

                def then(ins):
                    ins.then_inc(prep, 1)
                    steps[0] += 1
                    dve.wait_ge(prep, steps[0])

                dve.wait_ge(summed, 2)
                then(dve.tensor_scalar(w_mean[:], sum_ps[:, 0:2], 1.0 / (HID * D), 1e-5, ALU.mult, ALU.max))
                then(dve.reciprocal(w_scale[:], w_mean[:]))
                then(dve.reciprocal(w_mean[:], w_scale[:]))
                for w, src, t in ((1, w2_raw, weights.t2), (0, w1_raw, weights.t1)):
                    scale = w_scale[:, w:w + 1]
                    then(dve.tensor_scalar(above[:], src[:], scale, 0.5, ALU.mult, ALU.is_gt))
                    then(dve.tensor_scalar(below[:], src[:], scale, -0.5, ALU.mult, ALU.is_lt))
                    dve.tensor_tensor(t[:].rearrange("p c n -> p (c n)"), above[:], below[:], ALU.subtract)\
                        .then_inc(ternary, 1)
                    dve.wait_ge(ternary, 2 - w)
                dve.wait_ge(vec_in, 48)
                then(dve.tensor_scalar(b1_scaled[:], b1_raw[:], w_scale[0:2, 0:1], None, ALU.mult))
                then(dve.tensor_copy(b1_hi[:], b1_scaled[:]))
                then(dve.tensor_tensor(b1_parts[:], b1_scaled[:], b1_hi[:].bitcast(F32), ALU.subtract))
                dve.tensor_copy(b1_parts[0:1], b1_hi[0:1].bitcast(F32))
                dve.tensor_copy(weights.two_ones[:], ones[0:2])
                dve.wait_ge(shifted, 1)
                dve.scalar_tensor_tensor(weights.shift_row[:], n2_ps[:, 0:D], w_mean[:, 1:2], b2_row[:],
                                         ALU.mult, ALU.add)

            @block.tensor
            def _(pe):
                pe.wait_ge(const, 3)
                with pe.Fori(0, B // RING) as i:
                    for r in range(RING):
                        b, v = RING * i + r, r % 2
                        pe.wait_ge(copied, b + 1)
                        pe.wait_ge(normed, b + 1 + ahead[normed])
                        for c in range(DC):
                            for t in range(QT):
                                last = pe.transpose(ps[:, v, c, t * P:(t + 1) * P],
                                                    xn[:, v, t, c * P:(c + 1) * P], ident[:])
                        last.then_inc(turned, 1)
                for w in range(2):
                    pe.wait_ge(absed, w + 1)
                    pe.matmul(sum_ps[:, w:w + 1], ones[:], abs_part[:, w:w + 1], start=True,
                              stop=True).then_inc(summed, 1)
                pe.wait_ge(n2_ready, 1)
                pe.wait_ge(ternary, 1)
                for c in range(HC):
                    last = pe.matmul(n2_ps[:, 0:D], n2_cols[:, c], weights.t2[:, c].bitcast(F32),
                                     start=c == 0, stop=c == HC - 1)
                last.then_inc(shifted, 1)

            @block.scalar
            def _(act):
                act.dma_start(w1_raw[:], w1T).then_inc(w_in, 16)
                act.dma_start(w2_raw[:], w2T).then_inc(w_in, 16)
                act.dma_start(n2_sb[:], n2).then_inc(vec_in, 16)
                for dst, src in ((b1_raw, b1), (b2_row, b2)):
                    act.dma_start(dst[:], src.unsqueeze(0).partition_broadcast(dst.shape[0])).then_inc(vec_in, 16)
                act.wait_ge(const, 2)
                act.wait_ge(vec_in, 48)
                for c in range(HC):
                    last = act.activation(n2_cols[:, c], ones[:], ACT.Copy, scale=n2_sb[:, c:c + 1])
                last.then_inc(n2_ready, 1)
                act.wait_ge(w_in, 32)
                act.activation(xnt[:].rearrange("p v c q -> p (v c q)"), w1_raw[:], ACT.Abs,
                               accum_out=abs_part[:, 0:1]).then_inc(absed, 1)
                act.wait_ge(absed, 1)
                act.activation(xnt[:].rearrange("p v c q -> p (v c q)"), w2_raw[:], ACT.Abs,
                               accum_out=abs_part[:, 1:2]).then_inc(absed, 1)
                act.wait_ge(absed, 2)
                with act.Fori(0, B // RING) as i:
                    for r in range(RING):
                        b, v = RING * i + r, r % 2
                        act.wait_ge(xn_stored[v], 16 * (2 * i + r // 2) + 16)
                        act.wait_ge(turned, b + 1 + ahead[turned])
                        act.activation(xnt[:, v], ps[:, v], ACT.Copy).then_inc(copied, 1)
                        act.wait_ge(added, b + 1 + ahead[added])
                        act.dma_start(y[bass.ds(b, 1)].rearrange("o p t d -> p (o t) d"),
                                      yrow[:, v]).then_inc(y_stored[v], 16)
                        act.wait_ge(copied, b + 1 + ahead[copied])
                        act.dma_start(xnT[bass.ds(b, 1)].rearrange("o p c q -> p (o c) q"),
                                      xnt[:, v]).then_inc(xn_stored[v], 16)


def attention_stage(nc, ctxT, mask, wq, wk, wv, wo, xnT, y):
    with ExitStack() as ctx:
        sb = lambda name, shape, dt=F32: ctx.enter_context(nc.sbuf_tensor(name, shape, dt))
        sem = lambda name: ctx.enter_context(nc.semaphore(name))
        raw = sb("raw", [P, RAW, 512])
        ctx_hi, ctx_lo = (sb(f"ctx_{x}", [P, NH * DC, 512], F32R) for x in ("hi", "lo"))
        xn_hi, xn_lo = (sb(f"xn_{x}", [P, DC, NQ], F32R) for x in ("hi", "lo"))
        wq_hi, wq_lo = (sb(f"wq_{x}", [P, DC, QUAD * DH], F32R) for x in ("hi", "lo"))
        wk_hi, wk_lo = (sb(f"wk_{x}", [P, DC, QUAD * DH], F32R) for x in ("hi", "lo"))
        wv_hi, wv_lo = (sb(f"wv_{x}", [P, DC, QUAD * DH], F32R) for x in ("hi", "lo"))
        wo_hi, wo_lo = (sb(f"wo_{x}", [P, PAIR, D], F32R) for x in ("hi", "lo"))
        qp_hi, qp_lo = (sb(f"q_pair_{x}", [P, NQ], F32R) for x in ("hi", "lo"))
        q_hi, q_lo = (sb(f"q_{x}", [P, QUAD, NQ], F32R) for x in ("hi", "lo"))
        k_st = sb("k_stack", [P, QUAD, NKV], F32R)
        v_raw = sb("v_raw", [P, KC, QUAD, DH])
        v_st = sb("v_stack", [P, QUAD, KC, 2, DH], F32R)
        probs = sb("probs", [P, 2 * QT, NKV])
        pt_hi, pt_lo = (sb(f"pt_{x}", [P, 4, NQ], F32R) for x in ("hi", "lo"))
        u_half, u_raw = sb("u_half", [P, NQ]), sb("u_raw", [P, PAIR, NQ])
        u_hi, u_lo = (sb(f"u_{x}", [P, PAIR, NQ], F32R) for x in ("hi", "lo"))
        y_sb = sb("y_sb", [P, QT, D])
        mask_raw = sb("mask_raw", [P, NKV], U8)
        mask_bias = sb("mask_bias", [P, 2, NKV], BF16)
        low = sb("low", [P, SLOTS])
        rowsum, rinv = sb("rowsum", [P, SLOTS]), sb("rinv", [P, SLOTS])
        ident = sb("ident", [P, P])
        s_ps = ctx.enter_context(nc.psum_tensor("s_ps", [P, 2, NH, 512], F32))
        t_ps = ctx.enter_context(nc.psum_tensor("t_ps", [P, 2, NQ], F32))
        pv_ps = ctx.enter_context(nc.psum_tensor("pv_ps", [P, NQ], F32))
        m_ps = ctx.enter_context(nc.psum_tensor("m_ps", [P, 512], F32))

        ident0, ident_ready = sem("ident0"), sem("ident_ready")
        loaded = {j: sem(f"loaded_{j[0]}{j[2]}") for j in LOADS}
        split = {k: sem(f"split_{k}") for k in PIECES}
        unit = {k: sem(f"unit_{k}") for k in PER_QUAD}
        unit_hi = {k: sem(f"unit_hi_{k}") for k in "kq"}
        done = {k: sem(f"done_{k}") for k in PER_QUAD}
        k_lo_a = sem("k_lo_a")
        scored, masked, exped = sem("scored"), sem("masked"), sem("exped")
        inverted, normed = sem("inverted"), sem("normed")
        turned, t_hi, t_lo = sem("turned"), sem("t_hi"), sem("t_lo")
        pv = sem("pv")
        q_copied = [sem(f"q_copied{m}") for m in range(PAIR)]
        u_half_ready, u_ready = sem("u_half_ready"), sem("u_ready")
        mask_loaded, bias_ready = sem("mask_loaded"), sem("bias_ready")
        y_loaded, y_stored = sem("y_loaded"), sem("y_stored")

        passed_dve, passed_pool, passed_sp = sem("passed_dve"), sem("passed_pool"), sem("passed_sp")

        def unit_before(i, s):
            while True:
                s -= 1
                if isinstance(i, int) and i + s // SLOTS < -1:
                    return None
                if s % SLOTS in UNITS:
                    kind, dn, m = UNITS[s % SLOTS]
                    if valid(i, dn + s // SLOTS):
                        return kind, dn + s // SLOTS, m

        def unit_to_evacuate(s):
            if (s - 1) % SLOTS not in UNITS:
                return None
            kind, dn, m = UNITS[(s - 1) % SLOTS]
            return kind, dn + (s - 1) // SLOTS, m

        block = ctx.enter_context(nc.Block())

        @block.sync
        def _(sp):
            def batch(n):
                return bass.ds(n // QUADS, 1) if not isinstance(n, int) else slice(n // QUADS, n // QUADS + 1)

            def quad(n):
                return bass.ds(n % QUADS, 1) if not isinstance(n, int) else slice(n % QUADS, n % QUADS + 1)

            def free_buffer(i, p):
                r, before = 0, p - RAW
                while True:
                    if before < 0:
                        r, before = r - 1, max(x for x in range(len(LOADS)) if x % RAW == p % RAW)
                    kind, dn, m = LOADS[before]
                    if isinstance(i, int) and i + r < -1:
                        return
                    if valid(i, dn + r):
                        wait(sp, split[kind], i, 2 * PIECES[kind], 2 * (PIECES[kind] * (dn + r) + m + 1))
                        return
                    before -= RAW

            def load(i, p):
                kind, dn, m = LOADS[p]
                if not valid(i, dn):
                    return
                free_buffer(i, p)
                n, dst = i + dn, raw[:, p % RAW]
                arrived = loaded[LOADS[p]]
                if kind == "ctx":
                    sp.dma_start(dst, ctxT[batch(n), :, m].rearrange("o p k -> p (o k)")).then_inc(arrived, 16)
                elif kind == "xn":
                    sp.dma_start(dst, xnT[batch(n), :, m].rearrange("o p q -> p (o q)")).then_inc(arrived, 16)
                else:
                    w = {"wq": wq, "wk": wk, "wv": wv, "wo": wo}[kind]
                    sp.dma_start(dst, w[quad(n)].rearrange("o p n -> p (o n)")).then_inc(arrived, 16)

            def double_queries(i, dn, m):
                if not valid(i, dn):
                    return
                wait(sp, done["q"], i, PAIR, PAIR * dn + m + 1)
                for pair, dst in ((qp_hi, q_hi), (qp_lo, q_lo)):
                    for h in range(2):
                        src = pair[h * DH:(h + 1) * DH].bitcast(F32)
                        for half in range(2):
                            sp.dma_start(dst[half * DH:(half + 1) * DH, 2 * m + h].bitcast(F32), src)                                .then_inc(q_copied[m], 16)

            def body(i):
                load(i, 0)
                load(i, 1)
                if valid(i, -1):
                    wait(sp, y_stored, i, 16, 0)
                    sp.dma_start(y_sb[:], y[batch(i - 1)].rearrange("o p t d -> p (o t) d")).then_inc(y_loaded, 16)
                if valid(i, 1):
                    wait(sp, bias_ready, i, 2, 2)
                    stand_alone(sp, passed_sp)
                    sp.dma_start(mask_raw[:], mask[batch(i + 1), :].partition_broadcast(P)).then_inc(mask_loaded, 16)
                for p in range(2, len(LOADS)):
                    load(i, p)
                    if p == 4:
                        double_queries(i, 0, 1)
                    if p == 8:
                        double_queries(i, 1, 0)
                if valid(i, -1):
                    wait(sp, done["o"], i, 2, 0)
                    sp.dma_start(y[batch(i - 1)].rearrange("o p t d -> p (o t) d"), y_sb[:]).then_inc(y_stored, 16)

            sp.sem_inc(y_stored, 16)
            run_loop(sp, body, -1, STEPS)
            sp.wait_ge(y_stored, 16 * (STEPS + 1))

        @block.gpsimd
        def _(pool):
            pool.memset(ident[:], 0.0).then_inc(ident0, 1)
            pool.wait_ge(ident0, 1)
            pool.affine_select(out=ident[:], in_=ident[:], compare_op=ALU.not_equal, fill=1.0, base=0,
                               pattern=[[-1, P]], channel_multiplier=1).then_inc(ident_ready, 1)

            def operands(job):
                kind, _, m = job
                if kind == "vs":
                    return v_raw[:, :, m], v_st[:, m, :, 0], v_st[:, m, :, 1]
                if kind == "us":
                    return u_raw[:, m], u_hi[:, m], u_lo[:, m]
                src = raw[:, LOADS.index(job) % RAW]
                if kind == "ctx":
                    return src, ctx_hi[:, m], ctx_lo[:, m]
                if kind == "xn":
                    return src, xn_hi[:, m], xn_lo[:, m]
                hi, lo = {"wq": (wq_hi, wq_lo), "wk": (wk_hi, wk_lo), "wv": (wv_hi, wv_lo), "wo": (wo_hi, wo_lo)}[kind]
                return src.rearrange("p (c n) -> p c n", c=hi.shape[1]), hi[:], lo[:]

            def before_split(i, kind, dn, m):
                if kind == "vs":
                    if m == 0:
                        wait(pool, done["v"], i, 4, 4 * dn + 4)
                    wait(pool, pv, i, 32, 32 * (dn - 1) + KC * (m + 1))
                    return
                if kind == "us":
                    wait(pool, u_ready, i, QUAD, QUAD * dn + 2 * (m + 1))
                    return
                wait(pool, loaded[kind, dn, m], i, 16, 16 * (dn + 1) if dn >= 0 else 0)
                if kind == "wo":
                    wait(pool, unit["o"], i, 2, 2 * dn)
                if kind == "wk" or (kind == "ctx" and m == 0):
                    wait(pool, unit["k"], i, 4, 4 * dn)
                if kind == "wq" or (kind == "xn" and m == 0):
                    wait(pool, unit["q"], i, 2, 2 * dn)
                if kind == "wv":
                    wait(pool, unit["v"], i, 4, 4 * dn)

            def body(i):
                for s in range(SLOTS):
                    jobs = [j for j in JOBS.get(s, []) if valid(i, j[1])]
                    for kind, dn, m in jobs:
                        before_split(i, kind, dn, m)
                        src, hi, lo = operands((kind, dn, m))
                        stand_alone(pool, passed_pool)
                        pool.tensor_scalar(hi, src, 1.0, 1.0, ALU.mult, ALU.mult).then_inc(split[kind], 1)
                    for kind, dn, m in jobs:
                        src, hi, lo = operands((kind, dn, m))
                        wait(pool, split[kind], i, 2 * PIECES[kind], 2 * (PIECES[kind] * dn + m) + 1)
                        pool.tensor_tensor(lo, src, hi.bitcast(F32), ALU.subtract).then_inc(split[kind], 1)
                    if s == 12 and valid(i, 1):
                        wait(pool, mask_loaded, i, 16, 32)
                        wait(pool, masked, i, SLOTS, 8)
                        stand_alone(pool, passed_pool)
                        pool.tensor_scalar(mask_bias[:, 0], mask_raw[:], -MASKED, MASKED, ALU.mult,
                                           ALU.add).then_inc(bias_ready, 1)
                    if s == 2 and valid(i, 0):
                        wait(pool, masked, i, SLOTS, 0)
                        stand_alone(pool, passed_pool)
                        pool.tensor_scalar(mask_bias[:, 1], mask_raw[:], -MASKED, MASKED, ALU.mult,
                                           ALU.add).then_inc(bias_ready, 1)
                    dn, g, j = at_lag(s, 1)
                    if valid(i, dn):
                        t = QT * g + j
                        wait(pool, inverted, i, SLOTS, SLOTS * dn + t + 1)
                        tile = probs[:, t % (2 * QT)]
                        stand_alone(pool, passed_pool)
                        pool.tensor_scalar(tile, tile, rinv[:, t:t + 1], 1.0, ALU.mult, ALU.mult).then_inc(normed, 1)

            run_loop(pool, body, -1, STEPS)

        @block.tensor
        def _(pe):
            def three(out, hi, lo, hi2, lo2, start, stop):
                pe.matmul(out, hi, hi2, start=start, stop=False)
                pe.matmul(out, hi, lo2, start=False, stop=False)
                return pe.matmul(out, lo, hi2, start=False, stop=stop)

            def project(kind, m):
                if kind == "k":
                    pair, h = m // 2, m % 2
                    cols = slice(pair * P, (pair + 1) * P)
                    for c in range(DC):
                        last = three(m_ps[:], wk_hi[:, c, cols], wk_lo[:, c, cols], ctx_hi[:, h * DC + c],
                                     ctx_lo[:, h * DC + c], c == 0, c == DC - 1)
                elif kind == "q":
                    cols = slice(m * P, (m + 1) * P)
                    for c in range(DC):
                        last = three(m_ps[:], wq_hi[:, c, cols], wq_lo[:, c, cols], xn_hi[:, c], xn_lo[:, c],
                                     c == 0, c == DC - 1)
                elif kind == "v":
                    for r in range(2):
                        kc = 2 * m + r
                        h, keys = kc // 4, slice(kc % 4 * P, (kc % 4 + 1) * P)
                        for c in range(DC):
                            last = three(m_ps[:, r * D:(r + 1) * D], ctx_hi[:, h * DC + c, keys],
                                         ctx_lo[:, h * DC + c, keys], wv_hi[:, c], wv_lo[:, c],
                                         c == 0, c == DC - 1)
                else:
                    for r in range(2):
                        qs = slice((2 * m + r) * P, (2 * m + r + 1) * P)
                        for g in range(PAIR):
                            last = three(m_ps[:, r * D:(r + 1) * D], u_hi[:, g, qs], u_lo[:, g, qs],
                                         wo_hi[:, g], wo_lo[:, g], g == 0, g == PAIR - 1)
                return last

            def transpose_chunk(i, dn, g, j, r):
                c = KC * g + 2 * j + r
                wait(pe, t_lo, i, 32, 32 * dn + c - 1)
                if j == 0 and r == 0:
                    wait(pe, normed, i, SLOTS, SLOTS * dn + QT * (g + 1))
                for t in range(QT):
                    last = pe.transpose(t_ps[:, r, t * P:(t + 1) * P],
                                        probs[:, (QT * g + t) % (2 * QT), (2 * j + r) * P:(2 * j + r + 1) * P],
                                        ident[:])
                last.then_inc(turned, 1)

            def score(i, s):
                g, j = s // QT, s % QT
                wait(pe, exped, i, SLOTS, s - 1)
                if j == 0:
                    if g % 2 == 0:
                        wait(pe, q_copied[g // 2], i, 128, 128)
                        wait(pe, done["k"], i, 4, g + 2)
                qs = slice(j * P, (j + 1) * P)
                for part in (q_hi, q_lo):
                    for h in range(NH):
                        last = pe.matmul(s_ps[:, s % 2, h], part[:, g, qs], k_st[:, g, h * 512:(h + 1) * 512],
                                         start=part is q_hi, stop=part is q_lo)
                last.then_inc(scored, 1)

            def values(i, dn, g, j, turns):
                for r in range(2):
                    c = KC * g + 2 * j + r
                    if not turns:
                        wait(pe, t_lo, i, 32, 32 * dn + c + 1)
                    if j == 0 and r == 0:
                        wait(pe, u_ready, i, 4, 4 * dn + g)
                        wait(pe, split["vs"], i, 8, 2 * (4 * dn + g + 1))
                    lhsT = v_st[:, g, 2 * j + r].rearrange("p t d -> p (t d)")
                    pe.matmul(pv_ps[:], lhsT, pt_hi[:, c % 4], start=c % KC == 0, stop=False)
                    pe.matmul(pv_ps[:], lhsT, pt_lo[:, c % 4], start=False, stop=c % KC == KC - 1).then_inc(pv, 1)

            def ready(i, kind, dn, m):
                if kind == "k":
                    if m == 0:
                        wait(pe, split["wk"], i, 2, 2 * dn + 2)
                    if m < 2:
                        wait(pe, split["ctx"], i, 8, 8 * dn + 4 * (m + 1))
                elif kind == "q" and m == 0:
                    wait(pe, split["wq"], i, 2, 2 * dn + 2)
                    wait(pe, split["xn"], i, 4, 4 * dn + 4)
                elif kind == "v" and m == 0:
                    wait(pe, split["wv"], i, 2, 2 * dn + 2)
                elif kind == "o" and m == 0:
                    wait(pe, split["wo"], i, 2, 2 * dn + 2)
                    wait(pe, split["us"], i, 4, 4 * dn + 4)

            def body(i):
                for s in range(SLOTS):
                    dt, gt, jt = at_lag(s, T_LAG)
                    dv, gv, jv = at_lag(s, PV_LAG)
                    turns = valid(i, dt)
                    if turns:
                        transpose_chunk(i, dt, gt, jt, 0)
                    if valid(i, 0):
                        score(i, s)
                    if turns:
                        transpose_chunk(i, dt, gt, jt, 1)
                    if valid(i, dv):
                        values(i, dv, gv, jv, turns)
                    if s in UNITS and valid(i, UNITS[s][1]):
                        kind, dn, m = UNITS[s]
                        before = unit_before(i, s)
                        if before:
                            pk, pd, pm = before
                            wait(pe, done[pk], i, PER_QUAD[pk], PER_QUAD[pk] * pd + pm + 1)
                        ready(i, kind, dn, m)
                        project(kind, m).then_inc(unit[kind], 1)

            pe.wait_ge(ident_ready, 1)
            run_loop(pe, body, -1, STEPS)

        @block.scalar
        def _(act):
            def evacuate(i, kind, dn, m):
                if kind == "o":
                    return
                n = PER_QUAD[kind] * dn + m
                wait(act, unit[kind], i, PER_QUAD[kind], n + 1)
                if kind == "k":
                    keys = slice(m % 2 * 512, (m % 2 + 1) * 512)
                    a = 2 * (m // 2)
                    act.activation(k_st[0:DH, a, keys], m_ps[0:DH], ACT.Copy).then_inc(unit_hi["k"], 1)
                    act.activation(k_st[DH:P, a + 1, keys], m_ps[DH:P], ACT.Copy).then_inc(unit_hi["k"], 1)
                elif kind == "q":
                    wait(act, q_copied[1 - m], i, 128, 128 * (dn + m))
                    act.activation(qp_hi[:], m_ps[:], ACT.Copy, scale=-DH ** -0.5).then_inc(unit_hi["q"], 1)
                else:
                    if m == 0:
                        wait(act, split["vs"], i, 8, 8 * dn)
                    act.activation(v_raw[:, 2 * m:2 * m + 2].rearrange("p c h d -> p c (h d)"),
                                   m_ps[:].rearrange("p (c n) -> p c n", c=2), ACT.Copy).then_inc(done["v"], 1)

            def chunk_hi(i, dn, g, j, r):
                c = KC * g + 2 * j + r
                wait(act, turned, i, 32, 32 * dn + c + 1)
                wait(act, pv, i, 32, 32 * dn + c - 3)
                act.activation(pt_hi[:, c % 4], t_ps[:, r], ACT.Copy).then_inc(t_hi, 1)

            def body(i):
                for s in range(SLOTS):
                    du, gu, ju = at_lag(s, U_LAG)
                    if ju == QT - 1 and valid(i, du):
                        wait(act, pv, i, 32, 32 * du + KC * (gu + 1))
                        own, other = (slice(0, DH), slice(DH, P)) if gu % 2 == 0 else (slice(DH, P), slice(0, DH))
                        wait(act, u_ready, i, 4, 4 * du + gu - 1)
                        act.activation(u_half[own], pv_ps[other], ACT.Copy).then_inc(u_half_ready, 1)
                    todo = unit_to_evacuate(s)
                    if todo and valid(i, todo[1]):
                        evacuate(i, *todo)
                    dt, gt, jt = at_lag(s, T_LAG)
                    if valid(i, dt):
                        chunk_hi(i, dt, gt, jt, 0)
                    de, ge, je = at_lag(s, 1)
                    if valid(i, de):
                        t = QT * ge + je
                        wait(act, masked, i, SLOTS, SLOTS * de + t + 1)
                        if je == 0:
                            wait(act, turned, i, 32, 32 * de + KC * (ge - 1))
                        act.activation(probs[:, t % (2 * QT)], s_ps[:, t % 2], ACT.Exp, bias=low[:, t:t + 1],
                                       scale=-1.0, accum_out=rowsum[:, t:t + 1]).then_inc(exped, 1)
                    if valid(i, dt):
                        chunk_hi(i, dt, gt, jt, 1)

            run_loop(act, body, -1, STEPS)

        @block.vector
        def _(dve):
            def evacuate(i, kind, dn, m):
                n = PER_QUAD[kind] * dn + m
                if kind == "k":
                    keys = slice(m % 2 * 512, (m % 2 + 1) * 512)
                    a = 2 * (m // 2)
                    wait(dve, unit_hi["k"], i, 8, 2 * n + 1)
                    dve.tensor_tensor(k_st[DH:P, a, keys], m_ps[0:DH], k_st[0:DH, a, keys].bitcast(F32),
                                      ALU.subtract).then_inc(k_lo_a, 1)
                    wait(dve, unit_hi["k"], i, 8, 2 * n + 2)
                    wait(dve, k_lo_a, i, 4, n + 1)
                    dve.tensor_tensor(k_st[0:DH, a + 1, keys], m_ps[DH:P], k_st[DH:P, a + 1, keys].bitcast(F32),
                                      ALU.subtract).then_inc(done["k"], 1)
                elif kind == "q":
                    wait(dve, unit_hi["q"], i, 2, n + 1)
                    dve.scalar_tensor_tensor(qp_lo[:], m_ps[:], -DH ** -0.5, qp_hi[:].bitcast(F32),
                                             ALU.mult, ALU.subtract).then_inc(done["q"], 1)
                elif kind == "o":
                    wait(dve, unit["o"], i, 2, n + 1)
                    if m == 0:
                        wait(dve, y_loaded, i, 16, 16 * (dn + 1))
                    dst = y_sb[:, 2 * m:2 * m + 2].rearrange("p t d -> p (t d)")
                    dve.tensor_tensor(dst, m_ps[:], dst, ALU.add).then_inc(done["o"], 1)

            def chunk_lo(i, dn, g, j, r):
                c = KC * g + 2 * j + r
                wait(dve, t_hi, i, 32, 32 * dn + c + 1)
                dve.tensor_tensor(pt_lo[:, c % 4], t_ps[:, r], pt_hi[:, c % 4].bitcast(F32),
                                  ALU.subtract).then_inc(t_lo, 1)

            def body(i):
                for s in range(SLOTS):
                    du, gu, ju = at_lag(s, U_LAG)
                    if ju == QT - 1 and valid(i, du):
                        own = slice(0, DH) if gu % 2 == 0 else slice(DH, P)
                        if gu < 2:
                            wait(dve, split["us"], i, 4, 4 * (du - 1) + 2)
                        wait(dve, u_half_ready, i, 4, 4 * du + gu + 1)
                        dve.tensor_tensor(u_raw[own, gu // 2], pv_ps[own], u_half[own], ALU.add).then_inc(u_ready, 1)
                    todo = unit_to_evacuate(s)
                    if todo and valid(i, todo[1]):
                        evacuate(i, *todo)
                    dt, gt, jt = at_lag(s, T_LAG)
                    if valid(i, dt):
                        chunk_lo(i, dt, gt, jt, 0)
                    if valid(i, 0):
                        wait(dve, scored, i, SLOTS, s + 1)
                        if s == 0:
                            wait(dve, bias_ready, i, 2, 1)
                        if s == 8:
                            wait(dve, bias_ready, i, 2, 2)
                        stand_alone(dve, passed_dve)
                        tile = s_ps[:, s % 2]
                        bias = mask_bias[:, s // 8].rearrange("p (h k) -> p h k", h=NH)
                        dve.tensor_tensor_reduce(out=tile, in0=tile, in1=bias, scale=1.0, scalar=LARGEST,
                                                 op0=ALU.add, op1=ALU.min,
                                                 accum_out=low[:, s:s + 1]).then_inc(masked, 1)
                    de, ge, je = at_lag(s, 1)
                    if valid(i, de):
                        t = QT * ge + je
                        wait(dve, exped, i, SLOTS, SLOTS * de + t + 1)
                        dve.reciprocal(rinv[:, t:t + 1], rowsum[:, t:t + 1]).then_inc(inverted, 1)
                    if valid(i, dt):
                        chunk_lo(i, dt, gt, jt, 1)

            run_loop(dve, body, -1, STEPS)


TILES = 2 * QT
PAIRS = B // 2
Y_LEAD, Z_LEAD, HN_LEAD, H_LEAD, PARTS_LEAD, YB_LEAD = 5, 4, 3, 2, 1, 3
STATS_LAG, NORM_LAG, TURN_LAG, DOWN_LAG, OUT_LAG = 1, 2, 3, 4, 5
STORE_LAG = 3


def feedforward_stage(nc, g1, n1, g2, weights, y, out):
    with ExitStack() as ctx:
        sb = lambda name, shape, dt=F32: ctx.enter_context(nc.sbuf_tensor(name, shape, dt))
        sem = lambda name: ctx.enter_context(nc.semaphore(name))
        t1, t2, shift_row = weights.t1, weights.t2, weights.shift_row
        ident, half = sb("ident_f", [P, P]), sb("half_f", [P, QT])
        g1_sb, n1_sb, g2_row = sb("g1_sb", [P, DC]), sb("n1_sb", [P, DC]), sb("g2_row", [P, HID])
        y_in, yb = sb("y_in", [P, 2, QT, D]), sb("yb", [P, 2, QT, D])
        z, hn, ht = sb("z", [P, 2, D]), sb("hn", [P, 2, D]), sb("ht", [P, 2, DC, P])
        ht_hi, ht_lo = sb("ht_hi", [P, 2, DC, P], F32R), sb("ht_lo", [P, 2, DC, P], F32R)
        act_out, gn, gm = sb("act_out", [P, 2, HID]), sb("gn", [P, 2, HID]), sb("gm", [P, 2, HID])
        gt_hi, gt_lo = sb("gt_hi", [P, 2, HC, P], F32R), sb("gt_lo", [P, 2, HC, P], F32R)
        g_stats, y_stats, z_stats = sb("g_stats", [P, 2, 2, 6]), sb("y_stats", [P, 2, 6]), sb("z_stats", [P, 2, 6])
        mv, var, rstd = sb("f_mv", [P, 2, 3, 2]), sb("f_var", [P, 2, 3]), sb("f_rstd", [P, 2, 3])
        gbias = sb("gbias", [P, 2])
        out_sb = sb("out_sb", [P, 2, QT, D])
        f_ps = ctx.enter_context(nc.psum_tensor("f_ps", [P, 2, HID], F32))
        g_ps = ctx.enter_context(nc.psum_tensor("g_ps", [P, HC, P], F32))
        h_ps = ctx.enter_context(nc.psum_tensor("h_ps", [P, 512], F32))
        o_ps = ctx.enter_context(nc.psum_tensor("o_ps", [P, 512], F32))

        vec_in, y_in_s = sem("f_vec_in"), [sem("y_in_s0"), sem("y_in_s1")]
        ident0, const = sem("f_ident0"), sem("f_const")
        z_ready, hn_ready, yb_ready = sem("z_ready"), sem("hn_ready"), sem("yb_ready")
        stat, aggr, vared, rstded = sem("f_stat"), sem("f_aggr"), sem("f_vared"), sem("f_rstded")
        h_turned, h_taken, h_hi, h_lo = sem("h_turned"), sem("h_taken"), sem("h_hi"), sem("h_lo")
        up, gelued, gbiased, mv_set = sem("up"), sem("gelued"), sem("gbiased"), sem("mv_set")
        gn_ready, gm_ready, g_turned, g_hi, g_lo = (sem(x) for x in ("gn_ready", "gm_ready", "g_turned", "g_hi", "g_lo"))
        down, out_ready, out_stored = sem("down"), sem("out_ready"), [sem("out_stored0"), sem("out_stored1")]

        passed = sem("f_passed")

        def tile_ok(i, s, lag):
            return not isinstance(i, int) or 0 <= TILES * i + s - lag < B * QT

        def stats_ok(i, s):
            return not isinstance(i, int) or -Y_LEAD <= TILES * i + s < B * QT + STATS_LAG

        def stats_done(s):
            return s + Y_LEAD + 1

        def loop(eng, body):
            body(-1)
            body(0)
            with eng.Fori(1, PAIRS - 1) as i:
                body(i)
            body(PAIRS - 1)
            body(PAIRS)

        block = ctx.enter_context(nc.Block())

        @block.sync
        def _(sp):
            for u in range(2):
                sp.sem_inc(out_stored[u], 16)
            for dst, src in ((g1_sb, g1), (n1_sb, n1), (g2_row, g2.unsqueeze(0).partition_broadcast(P))):
                sp.dma_start(dst[:], src).then_inc(vec_in, 16)

            def body(i):
                for n in (1, 2):
                    b = 2 * i + n
                    if not isinstance(i, int) or 0 <= b < B:
                        wait(sp, z_ready, i, TILES, QT * (n - 1))
                        wait(sp, yb_ready, i, TILES, QT * (n - 1))
                        src = y[b:b + 1] if isinstance(i, int) else y[bass.ds(b, 1)]
                        sp.dma_start(y_in[:, n % 2], src.rearrange("o p t d -> p (o t) d")).then_inc(y_in_s[n % 2], 16)
                    if not isinstance(i, int) or 0 <= b - STORE_LAG < B:
                        wait(sp, out_ready, i, TILES, QT * (n - STORE_LAG + 1))
                        dst = out[b - STORE_LAG:b - STORE_LAG + 1] if isinstance(i, int) else out[bass.ds(b - STORE_LAG, 1)]
                        u = (n - STORE_LAG) % 2
                        sp.dma_start(dst.rearrange("o (t p) d -> p (o t) d", p=P), out_sb[:, u])\
                            .then_inc(out_stored[u], 16)

            body(-1)
            body(0)
            body(1)
            with sp.Fori(2, PAIRS - 1) as i:
                body(i)
            body(PAIRS - 1)
            body(PAIRS)
            for u in range(2):
                sp.wait_ge(out_stored[u], 16 * (PAIRS + 1))

        @block.gpsimd
        def _(pool):
            pool.memset(half[:], -0.5).then_inc(const, 1)
            pool.memset(ident[:], 0.0).then_inc(ident0, 1)
            pool.wait_ge(ident0, 1)
            pool.affine_select(out=ident[:], in_=ident[:], compare_op=ALU.not_equal, fill=1.0, base=0,
                               pattern=[[-1, P]], channel_multiplier=1).then_inc(const, 1)
            pool.wait_ge(const, 1)

            def body(i):
                for s in range(TILES):
                    if tile_ok(i, s, NORM_LAG):
                        r = (s - NORM_LAG) % 2
                        k = s - NORM_LAG + 1
                        if isinstance(i, int) and TILES * i + k == 1:
                            pool.wait_ge(vec_in, 48)
                        wait(pool, gn_ready, i, TILES, k)
                        wait(pool, g_turned, i, TILES, k - 2)
                        pool.tensor_tensor(gm[:, r], gn[:, r], g2_row[:], ALU.mult).then_inc(gm_ready, 1)
                    if stats_ok(i, s):
                        wait(pool, vared, i, TILES, stats_done(s))
                        pool.tensor_tensor(rstd[:, s % 2], var[:, s % 2], half[:, 0:3], ALU.pow).then_inc(rstded, 1)
                    if tile_ok(i, s, -PARTS_LEAD):
                        x = s + PARTS_LEAD
                        wait(pool, h_hi, i, TILES, x + 1)
                        pool.tensor_tensor(ht_lo[:, x % 2], ht[:, x % 2], ht_hi[:, x % 2].bitcast(F32),
                                           ALU.subtract).then_inc(h_lo, 1)
                    if tile_ok(i, s, -YB_LEAD):
                        x = s + YB_LEAD
                        v, t = x // QT % 2, x % QT
                        wait(pool, y_in_s[v], i, 16, 16 * (x // TILES + 1))
                        wait(pool, out_ready, i, TILES, x - TILES + 1)
                        pool.tensor_tensor(yb[:, v, t], y_in[:, v, t], shift_row[:], ALU.add).then_inc(yb_ready, 1)

            loop(pool, body)

        @block.tensor
        def _(pe):
            pe.wait_ge(const, 2)

            def body(i):
                for s in range(TILES):
                    if tile_ok(i, s, TURN_LAG):
                        r = (s - TURN_LAG) % 2
                        wait(pe, gm_ready, i, TILES, s - TURN_LAG + 1)
                        wait(pe, g_lo, i, TILES, s - TURN_LAG)
                        for c in range(HC):
                            last = pe.transpose(g_ps[:, c], gm[:, r, c * P:(c + 1) * P], ident[:])
                        last.then_inc(g_turned, 1)
                    if tile_ok(i, s, -H_LEAD):
                        x = s + H_LEAD
                        wait(pe, hn_ready, i, TILES, x + 1)
                        wait(pe, h_taken, i, TILES, x)
                        for c in range(DC):
                            last = pe.transpose(h_ps[:, c * P:(c + 1) * P], hn[:, x % 2, c * P:(c + 1) * P], ident[:])
                        last.then_inc(h_turned, 1)
                    if tile_ok(i, s, 0):
                        wait(pe, h_lo, i, TILES, s + 1)
                        wait(pe, gelued, i, TILES, s - 1)
                        for c in range(DC):
                            for part in (ht_hi, ht_lo):
                                for h in range(2):
                                    pe.matmul(f_ps[:, s % 2, h * 512:(h + 1) * 512], part[:, s % 2, c],
                                              t1[:, c, h * 512:(h + 1) * 512],
                                              start=c == 0 and part is ht_hi, stop=False)
                        for h in range(2):
                            last = pe.matmul(f_ps[:, s % 2, h * 512:(h + 1) * 512], weights.two_ones[:],
                                             weights.b1_parts[:, h * 512:(h + 1) * 512], start=False, stop=True)
                        last.then_inc(up, 1)
                    if tile_ok(i, s, DOWN_LAG):
                        r = (s - DOWN_LAG) % 2
                        wait(pe, g_lo, i, TILES, s - DOWN_LAG + 1)
                        wait(pe, out_ready, i, TILES, s - DOWN_LAG)
                        for c in range(HC):
                            pe.matmul(o_ps[:, 0:D], gt_hi[:, r, c], t2[:, c], start=c == 0, stop=False)
                            last = pe.matmul(o_ps[:, 0:D], gt_lo[:, r, c], t2[:, c], start=False, stop=c == HC - 1)
                        last.then_inc(down, 1)

            loop(pe, body)

        @block.scalar
        def _(act):
            act.wait_ge(vec_in, 48)

            def body(i):
                for s in range(TILES):
                    if tile_ok(i, s, NORM_LAG):
                        r = (s - NORM_LAG) % 2
                        k = s - NORM_LAG + 1
                        wait(act, gbiased, i, TILES, k)
                        wait(act, gm_ready, i, TILES, k - 2)
                        act.activation(gn[:, r], act_out[:, r], ACT.Identity, bias=gbias[:, r:r + 1],
                                       scale=rstd[:, (s - 1) % 2, 0:1]).then_inc(gn_ready, 1)
                    if tile_ok(i, s, TURN_LAG):
                        r = (s - TURN_LAG) % 2
                        k = s - TURN_LAG + 1
                        wait(act, g_turned, i, TILES, k)
                        wait(act, down, i, TILES, k - 2)
                        act.activation(gt_hi[:, r], g_ps[:], ACT.Copy).then_inc(g_hi, 1)
                    if tile_ok(i, s, -H_LEAD):
                        x = s + H_LEAD
                        wait(act, h_turned, i, TILES, x + 1)
                        wait(act, h_lo, i, TILES, x - 1)
                        for c in range(DC):
                            last = act.activation(ht[:, x % 2, c], h_ps[:, c * P:(c + 1) * P], ACT.Identity,
                                                  bias=n1_sb[:, c:c + 1], scale=g1_sb[:, c:c + 1])
                        last.then_inc(h_taken, 1)
                    if tile_ok(i, s, 0):
                        wait(act, gn_ready, i, TILES, s - 1)
                        wait(act, up, i, TILES, s + 1)
                        act.activation(act_out[:, s % 2], f_ps[:, s % 2], ACT.Gelu,
                                       scale=weights.scale[:, 0:1]).then_inc(gelued, 1)

            loop(act, body)

        @block.vector
        def _(dve):
            dve.memset(mv[:], 1.0).then_inc(mv_set, 1)
            dve.wait_ge(mv_set, 1)

            def normalize(dst, rows, s, kind):
                q = (s - 1) % 2
                return dve.tensor_scalar(dst, rows, mv[:, q, kind, 0:1], rstd[:, q, kind:kind + 1],
                                         ALU.subtract, ALU.mult)

            def body(i):
                for s in range(TILES):
                    q = s % 2
                    if tile_ok(i, s, OUT_LAG):
                        x = (s - OUT_LAG) % TILES
                        u, t = x // QT % 2, x % QT
                        wait(dve, down, i, TILES, s - OUT_LAG + 1)
                        wait(dve, yb_ready, i, TILES, s - OUT_LAG + 1)
                        if t == 0:
                            wait(dve, out_stored[u], i, 16, 16 * ((s - OUT_LAG) // TILES + 1))
                        dve.scalar_tensor_tensor(out_sb[:, u, t], o_ps[:, 0:D], weights.scale[:, 1:2], yb[:, u, t],
                                                 ALU.mult, ALU.add).then_inc(out_ready, 1)
                    if stats_ok(i, s - 1):
                        wait(dve, rstded, i, TILES, stats_done(s - 1))
                    if tile_ok(i, s, -Z_LEAD):
                        x = s + Z_LEAD
                        wait(dve, hn_ready, i, TILES, x - 1)
                        normalize(z[:, x % 2], y_in[:, x // QT % 2, x % QT], s, 1).then_inc(z_ready, 1)
                    if tile_ok(i, s, -HN_LEAD):
                        x = s + HN_LEAD
                        wait(dve, h_turned, i, TILES, x - 1)
                        normalize(hn[:, x % 2], z[:, x % 2], s, 2).then_inc(hn_ready, 1)
                    if tile_ok(i, s, -PARTS_LEAD):
                        x = s + PARTS_LEAD
                        wait(dve, h_taken, i, TILES, x + 1)
                        wait(dve, up, i, TILES, x - 1)
                        dve.tensor_copy(ht_hi[:, x % 2], ht[:, x % 2]).then_inc(h_hi, 1)
                    if stats_ok(i, s):
                        if tile_ok(i, s, -Y_LEAD):
                            x = s + Y_LEAD
                            v = x // QT % 2
                            wait(dve, y_in_s[v], i, 16, 16 * (x // TILES + 1))
                            last = dve.bn_stats(y_stats[:, q], y_in[:, v, x % QT])
                        if tile_ok(i, s, -Z_LEAD):
                            wait(dve, z_ready, i, TILES, s + Z_LEAD + 1)
                            last = dve.bn_stats(z_stats[:, q], z[:, (s + Z_LEAD) % 2])
                        if tile_ok(i, s, STATS_LAG):
                            wait(dve, gelued, i, TILES, s - STATS_LAG + 1)
                            r = (s - STATS_LAG) % 2
                            for h in range(2):
                                last = dve.bn_stats(g_stats[:, q, h], act_out[:, r, h * 512:(h + 1) * 512])
                        last.then_inc(stat, 1)
                        wait(dve, stat, i, TILES, stats_done(s))
                        stand_alone(dve, passed)
                        if tile_ok(i, s, STATS_LAG):
                            last = dve.bn_aggr(mv[:, q, 0], g_stats[:, q])
                        if tile_ok(i, s, -Y_LEAD):
                            last = dve.bn_aggr(mv[:, q, 1], y_stats[:, q])
                        if tile_ok(i, s, -Z_LEAD):
                            last = dve.bn_aggr(mv[:, q, 2], z_stats[:, q])
                        last.then_inc(aggr, 1)
                        wait(dve, aggr, i, TILES, stats_done(s))
                        dve.tensor_scalar(var[:, q], mv[:, q, :, 1], EPS, None, ALU.add).then_inc(vared, 1)
                    if tile_ok(i, s, TURN_LAG):
                        r = (s - TURN_LAG) % 2
                        wait(dve, g_hi, i, TILES, s - TURN_LAG + 1)
                        dve.tensor_tensor(gt_lo[:, r], g_ps[:], gt_hi[:, r].bitcast(F32),
                                          ALU.subtract).then_inc(g_lo, 1)
                    if tile_ok(i, s, STATS_LAG):
                        r = (s - STATS_LAG) % 2
                        wait(dve, rstded, i, TILES, stats_done(s))
                        dve.scalar_tensor_tensor(gbias[:, r:r + 1], mv[:, q, 0, 0:1], -1.0, rstd[:, q, 0:1],
                                                 ALU.mult, ALU.mult).then_inc(gbiased, 1)

            loop(dve, body)


def build(nc, x, ctxT, mask, wq, wk, wv, wo, b_out, g1, n1, w1T, b1, g2, n2, w2T, b2, out):
    xnT = nc.dram_tensor("xn_scratch", (B, P, DC, NQ), F32, kind="Internal").ap()
    y = nc.dram_tensor("y_scratch", (B, P, QT, D), F32, kind="Internal").ap()
    with ExitStack() as ctx:
        weights = Weights(lambda name, shape, dt=F32: ctx.enter_context(nc.sbuf_tensor(name, shape, dt)))
        normalize_stage(nc, x, b_out, w1T, w2T, b1, n2, b2, weights, xnT, y)
        attention_stage(nc, ctxT, mask, wq, wk, wv, wo, xnT, y)
        feedforward_stage(nc, g1, n1, g2, weights, y, out)


def lay_out(inputs):
    import numpy as np

    get = {k: np.asarray(v) for k, v in inputs.items()}
    inner = HEADS * DH
    cols = QUAD * DH

    def quads(w):
        return np.ascontiguousarray(w.reshape(QUADS, cols, DC, P).transpose(0, 3, 2, 1)).reshape(QUADS, P, DC * cols)

    wkv = get["L0_xattn_Wkv"]
    return {
        "x": get["x"],
        "ctxT": np.ascontiguousarray(get["ctx_1024"].reshape(B, NH, 512, DC, P).transpose(0, 4, 1, 3, 2))
                  .reshape(B, P, NH * DC, 512),
        "mask": get["mask_BxS2_bf1"],
        "wq": quads(get["L0_xattn_Wq"]),
        "wk": quads(wkv[:inner]),
        "wv": quads(wkv[inner:]),
        "wo": np.ascontiguousarray(get["L0_xattn_Wout"].reshape(D, QUADS, PAIR, 2 * DH).transpose(1, 3, 2, 0))
                .reshape(QUADS, P, PAIR * D),
        "b_out": get["L0_xattn_b_out"],
        "g1": np.ascontiguousarray(get["L0_ffn_ln1_g"].reshape(DC, P).T),
        "n1": np.ascontiguousarray(get["L0_ffn_ln1_b"].reshape(DC, P).T),
        "w1T": np.ascontiguousarray(get["L0_ffn_w1"].reshape(HID, DC, P).transpose(2, 1, 0)).reshape(P, DC * HID),
        "b1": get["L0_ffn_b1"],
        "g2": get["L0_ffn_ln2_g"],
        "n2": np.ascontiguousarray(get["L0_ffn_ln2_b"].reshape(HC, P).T),
        "w2T": np.ascontiguousarray(get["L0_ffn_w2"].reshape(D, HC, P).transpose(2, 1, 0)).reshape(P, HC * D),
        "b2": get["L0_ffn_b2"],
    }


def kernel(**inputs):
    import numpy as np
    import concourse.bacc as bacc
    from concourse.bass_utils import run_bass_kernel_spmd

    nc = bacc.Bacc("TRN2", target_bir_lowering=False, num_devices=1)
    arrays, args = {}, []
    for name, a in lay_out(inputs).items():
        a = np.ascontiguousarray(a)
        arrays[f"in_{name}"] = a
        args.append(nc.dram_tensor(f"in_{name}", a.shape, mybir.dt.from_np(a.dtype), kind="ExternalInput").ap())
    args.append(nc.dram_tensor("out", (B, NQ, D), F32, kind="ExternalOutput").ap())
    build(nc, *args)
    r = run_bass_kernel_spmd(nc, [arrays], core_ids=[0])
    return r.results[0]["out"]
```
